# Optimizing a Trainium2 kernel written in Bass

```python
import numpy as np
import jax
import jax.numpy as jnp

def _softmax(x, axis=-1):
    return jax.nn.softmax(x, axis=axis)

def _gelu(x):
    return jax.nn.gelu(x, approximate=True)

def _silu(x):
    return jax.nn.silu(x)

def _sigmoid(x):
    return jax.nn.sigmoid(x)

def _layernorm(x, axis=-1, eps=1e-05):
    m = jnp.mean(x, axis=axis, keepdims=True)
    v = jnp.var(x, axis=axis, keepdims=True)
    return (x - m) / jnp.sqrt(v + eps)

def _scatter_add(tgt, idx, src, axis=0):
    return tgt.at[idx].add(src)

def _segment_sum(src, seg, n):
    return jax.ops.segment_sum(src, seg, n)
kernel_name = 'mk_adaln_d1_jaxref_r8_50d014'

def setup_inputs(seed: int=0):
    np.random.seed(seed)
    _w = jnp.asarray

    def _L0_attn_setup():
        import jax, jax.numpy as jnp
        import numpy as np
        ROPE_THETA = 10000.0

        def rope(t, rot_dim):
            S = t.shape[-2]
            half = rot_dim // 2
            inv_freq = 1.0 / ROPE_THETA ** (jnp.arange(0, rot_dim, 2, dtype=jnp.float32) / rot_dim)
            freqs = jnp.arange(S, dtype=jnp.float32)[:, None] * inv_freq[None, :]
            freqs = jnp.repeat(freqs, 2, axis=-1)
            cos, sin = (jnp.cos(freqs), jnp.sin(freqs))
            t_rot, t_pass = (t[..., :rot_dim], t[..., rot_dim:])
            x = t_rot.reshape(*t_rot.shape[:-1], half, 2)
            rh = jnp.stack([-x[..., 1], x[..., 0]], axis=-1).reshape(t_rot.shape)
            t_rot = t_rot * cos + rh * sin
            return jnp.concatenate([t_rot, t_pass], axis=-1)

        def feature_map(x):
            norm = jnp.sqrt(jnp.sum(x * x, axis=-1, keepdims=True))
            return x / jnp.maximum(norm, 1e-12)
        key = jax.random.key(seed)
        kx, kwi, kwo = jax.random.split(key, 3)
        B, S, D = (8, 512, 256)
        scale = 0.02
        return {'X': jax.random.normal(kx, (B, S, D), dtype=jnp.float32), 'W_in': jax.random.normal(kwi, (3 * D, D), dtype=jnp.float32) * scale, 'b_in': jnp.zeros((3 * D,), dtype=jnp.float32), 'W_out': jax.random.normal(kwo, (D, D), dtype=jnp.float32) * scale, 'b_out': jnp.zeros((D,), dtype=jnp.float32)}
    _L0_attn_in = _L0_attn_setup()

    def _L0_ffn_setup():
        import jax, jax.numpy as jnp
        import numpy as np
        EPS = 1e-08

        def _quantize(w):
            gamma = jnp.mean(jnp.abs(w))
            return jnp.clip(jnp.round(w / (gamma + EPS)), -1.0, 1.0)

        def _bitlinear(x, w):
            return jnp.matmul(x, _quantize(w).T)
        key = jax.random.key(seed)
        k1, k2, k3, k4 = jax.random.split(key, 4)
        d, h = (256, 704)
        x = jax.random.normal(k1, (4, 256, d), dtype=jnp.float32)
        w1 = jax.random.normal(k2, (h, d), dtype=jnp.float32)
        w2 = jax.random.normal(k3, (h, d), dtype=jnp.float32)
        w3 = jax.random.normal(k4, (d, h), dtype=jnp.float32)
        return {'x': x, 'w1': w1, 'w2': w2, 'w3': w3}
    _L0_ffn_in = _L0_ffn_setup()
    _L0_c = _w((lambda *s: np.random.randn(*s).astype(np.float32) * 0.05)(1, 256))
    _L0_wmod = _w((lambda *s: np.random.randn(*s).astype(np.float32) * 0.05)(256, 6 * 256) * 256 ** (-0.5))
    _d = {'L0_attn_X': _L0_attn_in['X'], 'L0_attn_W_in': _L0_attn_in['W_in'], 'L0_attn_b_in': _L0_attn_in['b_in'], 'L0_attn_W_out': _L0_attn_in['W_out'], 'L0_attn_b_out': _L0_attn_in['b_out'], 'L0_ffn_w1': _L0_ffn_in['w1'], 'L0_ffn_w2': _L0_ffn_in['w2'], 'L0_ffn_w3': _L0_ffn_in['w3'], 'L0_c': _L0_c, 'L0_wmod': _L0_wmod}
    _x0 = _d['L0_attn_X']
    _d['L0_attn_X'] = jax.random.normal(jax.random.fold_in(jax.random.key(seed), 1), (1, 1024, 256), dtype=_x0.dtype)
    del _x0
    return _d

def reference(L0_attn_X, L0_attn_W_in, L0_attn_b_in, L0_attn_W_out, L0_attn_b_out, L0_ffn_w1, L0_ffn_w2, L0_ffn_w3, L0_c, L0_wmod):

    def _L0_attn_ref(X, W_in, b_in, W_out, b_out):
        import jax, jax.numpy as jnp
        import numpy as np
        ROPE_THETA = 10000.0

        def rope(t, rot_dim):
            S = t.shape[-2]
            half = rot_dim // 2
            inv_freq = 1.0 / ROPE_THETA ** (jnp.arange(0, rot_dim, 2, dtype=jnp.float32) / rot_dim)
            freqs = jnp.arange(S, dtype=jnp.float32)[:, None] * inv_freq[None, :]
            freqs = jnp.repeat(freqs, 2, axis=-1)
            cos, sin = (jnp.cos(freqs), jnp.sin(freqs))
            t_rot, t_pass = (t[..., :rot_dim], t[..., rot_dim:])
            x = t_rot.reshape(*t_rot.shape[:-1], half, 2)
            rh = jnp.stack([-x[..., 1], x[..., 0]], axis=-1).reshape(t_rot.shape)
            t_rot = t_rot * cos + rh * sin
            return jnp.concatenate([t_rot, t_pass], axis=-1)

        def feature_map(x):
            norm = jnp.sqrt(jnp.sum(x * x, axis=-1, keepdims=True))
            return x / jnp.maximum(norm, 1e-12)
        D = X.shape[-1]
        QKV = jnp.einsum('bsd,ed->bse', X, W_in) + b_in
        Q, K, V = jnp.split(QKV, 3, axis=-1)
        rot_dim = D // 2
        Q = rope(Q, rot_dim)
        K = rope(K, rot_dim)
        A = jnp.sum(feature_map(K) * V, axis=-2)
        Y = A[:, None, :] * Q
        Y = jnp.einsum('bsd,ed->bse', Y, W_out) + b_out
        return Y + X

    def _L0_ffn_ref(x, w1, w2, w3):
        import jax, jax.numpy as jnp
        import numpy as np
        EPS = 1e-08

        def _quantize(w):
            gamma = jnp.mean(jnp.abs(w))
            return jnp.clip(jnp.round(w / (gamma + EPS)), -1.0, 1.0)

        def _bitlinear(x, w):
            return jnp.matmul(x, _quantize(w).T)
        x1 = _bitlinear(x, w1)
        x2 = _bitlinear(x, w2)
        hidden = jax.nn.sigmoid(x1) * x2
        return _bitlinear(hidden, w3)
    x = L0_attn_X
    mod = (_silu(L0_c) @ L0_wmod).reshape(L0_c.shape[0], 6, 1, -1)
    sa, ca, ga, sb, cb, gb = (mod[:, 0], mod[:, 1], mod[:, 2], mod[:, 3], mod[:, 4], mod[:, 5])
    ga = (2 * (ga >= 0) - 1) * jnp.maximum(jnp.abs(ga), 0.25)
    gb = (2 * (gb >= 0) - 1) * jnp.maximum(jnp.abs(gb), 0.25)
    h = _layernorm(x, axis=-1) * (1 + ca) + sa
    x = x + ga * _L0_attn_ref(h, L0_attn_W_in, L0_attn_b_in, L0_attn_W_out, L0_attn_b_out)
    h = _layernorm(x, axis=-1) * (1 + cb) + sb
    x = x + gb * _L0_ffn_ref(h, L0_ffn_w1, L0_ffn_w2, L0_ffn_w3)
    return x

_drawn_inputs = setup_inputs


def setup_inputs(seed=0):
    import zlib

    import numpy as np

    out = dict(_drawn_inputs(seed))
    spreads = {'L0_attn_b_in': (0.0, 0.1), 'L0_attn_b_out': (0.0, 0.1)}
    factors = {}
    for name, (base, spread) in spreads.items():
        noise = np.random.default_rng([zlib.crc32(name.encode()), seed]).standard_normal(out[name].shape)
        drawn = base * np.exp(spread * noise) if base else spread * noise
        out[name] = jnp.asarray(drawn.astype(out[name].dtype))
    for name, factor in factors.items():
        out[name] = (out[name] * factor).astype(out[name].dtype)
    return out
```

```python
from contextlib import ExitStack

import numpy as np

import concourse.bass as bass
from concourse import mybir

F32 = mybir.dt.float32
F32R = mybir.dt.float32r
ALU = mybir.AluOpType
ACT = mybir.ActivationFunctionType

P = 128
S, D = 1024, 256
TILES = S // P
KC = D // P
ROT = D // 2
HALF = ROT // 2
HID = 704
FULL = HID // P
REST = HID - FULL * P
HC = FULL + 1
NH = 2
HT = TILES // NH
N = S // NH
EPS = 1e-5
MIN_NORM = 1e-12
QUANT_EPS = 1e-8
MIN_GATE = 0.25
SA, CA, GA, SB, CB, GB = range(6)
NO_B = 2 * REST + FULL * P


def adaln_block(nc, x_in, w_in_t, b_in, b_q_cols, w_out_t, b_out_cols, w1_t, w2_t, w3_t, c_cols, wmod,
                cos_tok, sin_tok, cos_feat, sin_feat, ident_in, out):
    ctx = ExitStack()
    early = ExitStack()
    with ctx:
        def sb(name, shape, dt=F32):
            return ctx.enter_context(nc.sbuf_tensor(name, shape, dt))

        def early_sb(name, shape, dt=F32):
            return early.enter_context(nc.sbuf_tensor(name, shape, dt))

        def sem(name):
            return ctx.enter_context(nc.semaphore(name))

        x = sb("x", [P, TILES, D])
        w1 = sb("w1", [P, KC, HID])
        w2 = sb("w2", [P, KC, HID])
        w3 = sb("w3", [P, HC, D])
        c = sb("c", [P, KC])
        bq_in = sb("bq_in", [P, KC])
        bo_in = sb("bo_in", [P, KC])
        ident = sb("ident", [P, P])

        ones = sb("ones", [P, P])
        ones_r = sb("ones_r", [P, P], F32R)
        minus_half = sb("minus_half", [P, TILES])

        sig_c = sb("sig_c", [P, KC])
        silu_c = sb("silu_c", [P, KC])
        mod = sb("mod", [P, 6, KC])
        scale1 = sb("scale1", [P, KC])
        scale2 = sb("scale2", [P, KC])
        gate_sign = sb("gate_sign", [P, 2, KC])
        gate_neg = sb("gate_neg", [P, 2, KC])
        gate_size = sb("gate_size", [P, 2, KC])
        rows_src = sb("rows_src", [P, 4, KC])
        shift_t = sb("shift_t", [P, KC])
        rows = sb("rows", [P, 4, D])
        bq = sb("bq", [P, KC])

        stats = sb("stats", [P, TILES, 6])
        meanvar = sb("meanvar", [P, TILES, 2])
        var_eps = sb("var_eps", [P, TILES])
        rstd = sb("rstd", [P, TILES])
        stats2 = sb("stats2", [P, TILES, 6])
        meanvar2 = sb("meanvar2", [P, TILES, 2])
        var_eps2 = sb("var_eps2", [P, TILES])
        rstd2 = sb("rstd2", [P, TILES])
        xn = sb("xn", [P, TILES, D])
        x1 = sb("x1", [P, TILES, D])
        t_hi = sb("t_hi", [P, KC, S], F32R)
        t_lo = sb("t_lo", [P, KC, S], F32R)
        h2 = sb("h2", [P, KC, S])

        ssq = sb("ssq", [P, TILES])
        ssq_min = sb("ssq_min", [P, TILES])
        rnorm = sb("rnorm", [P, TILES])
        a = sb("a", [P, KC])
        wa = sb("wa", [P, KC, D])

        abs_sum = sb("abs_sum", [P, 3])
        thr = sb("thr", [P, 3])
        nthr = sb("nthr", [P, 3])
        above = sb("above", [P, 2 * P * HC])
        w12q = sb("w12q", [P, KC, 2 * HID], F32R)
        w3q = sb("w3q", [P, HC, D], F32R)

        w_in = early_sb("w_in", [P, KC, 3 * D])
        w_out = early_sb("w_out", [P, KC, D])
        wm = early_sb("wm", [P, KC, 6 * D])
        cosk = early_sb("cosk", [P, TILES, HALF])
        sink = early_sb("sink", [P, TILES, 2, HALF])
        cosq = early_sb("cosq", [P, S])
        sinq = early_sb("sinq", [P, S])
        brow_in = early_sb("brow_in", [P, 2 * D])
        sa_wide = early_sb("sa_wide", [P, KC, P])
        brow = early_sb("brow", [P, 2 * D])
        brow_r = early_sb("brow_r", [P, 2 * D], F32R)
        w_hi = early_sb("w_hi", [P, KC, 3 * D], F32R)
        w_lo = early_sb("w_lo", [P, KC, 3 * D], F32R)
        sq_junk = early_sb("sq_junk", [P, D])
        kv_in = early_sb("kv_in", [P, TILES, 2 * D])
        kc = early_sb("kc", [P, 4, 2, HALF])
        ks = early_sb("ks", [P, 4, 2, HALF])
        kr = early_sb("kr", [P, 4, 2, HALF])
        kv = early_sb("kv", [P, TILES, D])
        qc = early_sb("qc", [P, 2, N])
        qs = early_sb("qs", [P, 2, N])
        q = early_sb("q", [P, KC, S])
        absj = early_sb("absj", [P, 2 * P * HC])
        early.close()

        sig = sb("sig", [P, 3, N])
        hid = sb("hid", [P, 3, N])
        hid_hi = sb("hid_hi", [P, HC, S], F32R)
        hid_lo = sb("hid_lo", [P, HC, S], F32R)

        bank = [ctx.enter_context(nc.psum_tensor(f"bank{i}", [P, 512], F32)) for i in range(8)]
        misc = bank[7]
        MOD0, QB0, A0, G0 = 0, 16, 32, 48

        x_loaded = [sem(f"x_loaded{h}") for h in range(NH)]
        c_loaded, ident_loaded = sem("c_loaded"), sem("ident_loaded")
        wm_a_loaded, wm_b_loaded = sem("wm_a_loaded"), sem("wm_b_loaded")
        kv_w_loaded, q_w_loaded = sem("kv_w_loaded"), sem("q_w_loaded")
        brow_loaded, bcol_loaded = sem("brow_loaded"), sem("bcol_loaded")
        cosk_loaded, sink_loaded, ropeq_loaded = sem("cosk_loaded"), sem("sink_loaded"), sem("ropeq_loaded")
        w_out_loaded = sem("w_out_loaded")
        ffn_loaded = [sem(f"w{i + 1}_loaded") for i in range(3)]
        out_stored = sem("out_stored")

        brow_zeroed, w3_zeroed = sem("brow_zeroed"), sem("w3_zeroed")
        exponent_set, ones_set, pads_zeroed, sa_zeroed = (
            sem("exponent_set"), sem("ones_set"), sem("pads_zeroed"), sem("sa_zeroed"))
        sig_c_ready, silu_ready = sem("sig_c_ready"), sem("silu_ready")
        mod_a_summed, mod_b_summed = sem("mod_a_summed"), sem("mod_b_summed")
        mod_a_cols, mod_b_cols = sem("mod_a_cols"), sem("mod_b_cols")
        gates_part, gates_ready, shift_ready, rows_src_ready = (
            sem("gates_part"), sem("gates_ready"), sem("shift_ready"), sem("rows_src_ready"))
        rows_spread, rows_ready = sem("rows_spread"), sem("rows_ready")
        stats_ready, aggr_ready, var_ready, rstd_ready = (
            sem("stats_ready"), sem("aggr_ready"), sem("var_ready"), sem("rstd_ready"))
        xn_ready, xt_turned, t_hi_ready, t_lo_ready = (
            sem("xn_ready"), sem("xt_turned"), sem("t_hi_ready"), sem("t_lo_ready"))
        w_hi_ready, w_lo_ready = sem("w_hi_ready"), sem("w_lo_ready")
        brow_summed, brow_ready, brow_hi_ready, brow_lo_ready = (
            sem("brow_summed"), sem("brow_ready"), sem("brow_hi_ready"), sem("brow_lo_ready"))
        bq_summed, bq_ready = sem("bq_summed"), sem("bq_ready")
        kv_done, kv_in_ready, squares_done = sem("kv_done"), sem("kv_in_ready"), sem("squares_done")
        rope_k_parts, rope_k_ready, kv_pass_ready, kv_rot_ready = (
            sem("rope_k_parts"), sem("rope_k_ready"), sem("kv_pass_ready"), sem("kv_rot_ready"))
        ssq_min_ready, rnorm_ready = sem("ssq_min_ready"), sem("rnorm_ready")
        a_summed, a_ready, wa_ready = sem("a_summed"), sem("a_ready"), sem("wa_ready")
        q_rot_done, q_pass_done, q_parts, q_rot_ready, q_pass_ready = (
            sem("q_rot_done"), sem("q_pass_done"), sem("q_parts"), sem("q_rot_ready"), sem("q_pass_ready"))
        res_scaled, res_added, res_ready = sem("res_scaled"), sem("res_added"), sem("res_ready")
        y_done, x1_ready = sem("y_done"), sem("x1_ready")
        stats2_ready, aggr2_ready, var2_ready, rstd2_ready = (
            sem("stats2_ready"), sem("aggr2_ready"), sem("var2_ready"), sem("rstd2_ready"))
        xn2_ready, xt2_turned, h2_ready, h2_hi_ready, h2_lo_ready = (
            sem("xn2_ready"), sem("xt2_turned"), sem("h2_ready"), sem("h2_hi_ready"), sem("h2_lo_ready"))
        abs_done, gamma_summed, thr_ready, above_ready, quant_ready = (
            sem("abs_done"), sem("gamma_summed"), sem("thr_ready"), sem("above_ready"), sem("quant_ready"))
        up_done, sig_ready, hid_ready, hid_hi_ready, hid_lo_ready = (
            sem("up_done"), sem("sig_ready"), sem("hid_ready"), sem("hid_hi_ready"), sem("hid_lo_ready"))
        down_done, ffn_scaled, out_ready = sem("down_done"), sem("ffn_scaled"), sem("out_ready")

        def xt_bank(h, k):
            return bank[2 * h + k]

        def kv_bank(t):
            return bank[(4, 5, 0, 1)[t % 4]]

        q_bank = [(bank[2], bank[3]), (bank[4], bank[5])]
        y_bank = [bank[0], bank[1], bank[6], bank[2]]
        xt2_bank = [(bank[4], bank[5]), (bank[0], bank[1])]
        up_banks = [(bank[6], bank[7]), (bank[2], bank[3]), (bank[4], bank[5])]
        down_bank = [bank[0], bank[1], bank[0], bank[1]]

        def up_cols(j):
            return j * P, NO_B + j * P

        ORDER = [(h, j) for h in range(NH) for j in range(HC)]

        def cols(h):
            return slice(h * N, (h + 1) * N)

        block = ctx.enter_context(nc.Block())

        @block.sync
        def _(sp):
            xv = x_in.rearrange("(p t) d -> p t d", t=TILES)
            wv = w_in_t.rearrange("(k p) n -> p k n", p=P)
            sp.dma_start(x[:, 0:HT, :], xv[:, 0:HT, :]).then_inc(x_loaded[0], 16)
            sp.dma_start(w_in[:, :, 0:2 * D], wv[:, :, 0:2 * D]).then_inc(kv_w_loaded, 16)
            sp.dma_start(x[:, HT:TILES, :], xv[:, HT:TILES, :]).then_inc(x_loaded[1], 16)
            sp.wait_ge(brow_zeroed, 1)
            for r in (0, 32):
                sp.dma_start(brow_in[r:r + 1, :], b_in[:, 0:2 * D]).then_inc(brow_loaded, 16)
            sp.dma_start(w_in[:, :, 2 * D:], wv[:, :, 2 * D:]).then_inc(q_w_loaded, 16)
            sp.dma_start(cosk[:, :, :], cos_tok.rearrange("(p t) d -> p t d", t=TILES)).then_inc(cosk_loaded, 16)
            sp.dma_start(sink[:, :, :, :], sin_tok.rearrange("(p t) (a d) -> p t a d", t=TILES, a=2)
                         ).then_inc(sink_loaded, 16)
            sp.dma_start(cosq[:, :], cos_feat).then_inc(ropeq_loaded, 16)
            sp.dma_start(sinq[:, :], sin_feat).then_inc(ropeq_loaded, 16)
            sp.dma_start(w_out[:, :, :], w_out_t.rearrange("(k p) n -> p k n", p=P)).then_inc(w_out_loaded, 16)
            sp.wait_ge(w3_zeroed, 1)
            sp.dma_start(w3[:, 0:FULL, :], w3_t[0:FULL * P, :].rearrange("(k p) n -> p k n", p=P)
                         ).then_inc(ffn_loaded[2], 16)
            sp.dma_start(w3[0:REST, FULL, :], w3_t[FULL * P:, :]).then_inc(ffn_loaded[2], 16)
            ov = out.rearrange("(p t) d -> p t d", t=TILES)
            for i in range(TILES // 2):
                sp.wait_ge(out_ready, i + 1)
                sp.dma_start(ov[:, 2 * i:2 * i + 2, :], x[:, 2 * i:2 * i + 2, :]).then_inc(out_stored, 16)
            sp.wait_ge(out_stored, 16 * (TILES // 2))

        @block.scalar
        def _(act):
            act.dma_start(c[:, :], c_cols).then_inc(c_loaded, 16)
            wmv = wmod.rearrange("(k p) n -> p k n", p=P)
            act.dma_start(wm[:, :, 0:2 * D], wmv[:, :, 0:2 * D]).then_inc(wm_a_loaded, 16)
            act.dma_start(ident[:, :], ident_in).then_inc(ident_loaded, 16)
            act.dma_start(bq_in[:, :], b_q_cols).then_inc(bcol_loaded, 16)
            act.dma_start(bo_in[:, :], b_out_cols).then_inc(bcol_loaded, 16)
            act.dma_start(wm[:, :, 2 * D:], wmv[:, :, 2 * D:]).then_inc(wm_b_loaded, 16)
            for i, (dst, src) in enumerate(((w1, w1_t), (w2, w2_t))):
                act.dma_start(dst[:, :, :], src.rearrange("(k p) n -> p k n", p=P)).then_inc(ffn_loaded[i], 16)

            act.wait_ge(c_loaded, 16)
            nc.scalar.activation(sig_c[:, :], c[:, :], ACT.Sigmoid).then_inc(sig_c_ready, 1)

            act.wait_ge(kv_w_loaded, 16)
            act.wait_ge(mod_a_cols, 1)
            for k in range(KC):
                nc.scalar.activation(w_hi[:, k, 0:2 * D], w_in[:, k, 0:2 * D], ACT.Identity,
                                     scale=scale1[:, k:k + 1]).then_inc(w_hi_ready, 1)

            for h in range(NH):
                for k in range(KC):
                    act.wait_ge(xt_turned, KC * h + k + 1)
                    nc.scalar.activation(t_hi[:, k, cols(h)], xt_bank(h, k)[:, :], ACT.Identity
                                         ).then_inc(t_hi_ready, 1)
                if h == 0:
                    act.wait_ge(brow_ready, 1)
                    nc.scalar.activation(brow_r[:, :], brow[:, :], ACT.Identity).then_inc(brow_hi_ready, 1)
                    act.wait_ge(q_w_loaded, 16)
                    for k in range(KC):
                        nc.scalar.activation(w_hi[:, k, 2 * D:], w_in[:, k, 2 * D:], ACT.Identity,
                                             scale=scale1[:, k:k + 1]).then_inc(w_hi_ready, 1)

            def rows_out():
                for i in range(2):
                    act.wait_ge(rows_spread, i + 1)
                    nc.scalar.activation(rows[:, 2 * i:2 * i + 2, :], bank[2 + i][:, :], ACT.Identity
                                         ).then_inc(rows_ready, 1)

            def abs_sums(i):
                act.wait_ge(ffn_loaded[i], 32 if i == 2 else 16)
                if i == 2:
                    act.wait_ge(w3_zeroed, 1)
                if i > 0:
                    act.wait_ge(abs_done, i)
                w = (w1, w2, w3)[i]
                n = w.shape[1] * w.shape[2]
                nc.scalar.activation(absj[:, 0:n], w[:, :, :].rearrange("p k n -> p (k n)"), ACT.Abs,
                                     accum_out=abs_sum[:, i:i + 1]).then_inc(abs_done, 1)

            for t in range(TILES):
                act.wait_ge(kv_done, t + 1)
                nc.scalar.activation(kv_in[:, t, :], kv_bank(t)[:, :], ACT.Identity).then_inc(kv_in_ready, 1)
                act.wait_ge(kv_in_ready, t + 1)
                if t > 0:
                    act.wait_ge(squares_done, t)
                nc.scalar.activation(sq_junk[:, :], kv_in[:, t, 0:D], ACT.Square,
                                     accum_out=ssq[:, t:t + 1]).then_inc(squares_done, 1)
                if t == 1:
                    rows_out()
                if t in (2, 3, 4):
                    abs_sums(t - 2)

            for h in range(NH):
                act.wait_ge(q_pass_done, h + 1)
                act.wait_ge(bq_ready, 1)
                nc.scalar.activation(q[:, 1, cols(h)], q_bank[h][1][:, :], ACT.Identity, bias=bq[:, 1:2]
                                     ).then_inc(q_pass_ready, 1)

            act.wait_ge(mod_b_cols, 2)
            for h in range(NH):
                for k in range(KC):
                    act.wait_ge(xt2_turned, KC * h + k + 1)
                    nc.scalar.activation(h2[:, k, cols(h)], xt2_bank[h][k][:, :], ACT.Identity,
                                         bias=mod[:, SB, k:k + 1], scale=scale2[:, k:k + 1]).then_inc(h2_ready, 1)

            def hid_hi_part(n):
                h, j = ORDER[n]
                r = P if j < FULL else REST
                act.wait_ge(hid_ready, n + 1)
                nc.scalar.activation(hid_hi[0:r, j, cols(h)], hid[0:r, n % 3, :], ACT.Identity
                                     ).then_inc(hid_hi_ready, 1)

            for n, (h, j) in enumerate(ORDER):
                r = P if j < FULL else REST
                act.wait_ge(up_done, n + 1)
                if n >= 3:
                    act.wait_ge(hid_ready, n - 2)
                nc.scalar.activation(sig[0:r, n % 3, :], up_banks[n % 3][0][0:r, :], ACT.Sigmoid
                                     ).then_inc(sig_ready, 1)
                if n >= 1:
                    hid_hi_part(n - 1)
            hid_hi_part(len(ORDER) - 1)

        @block.vector
        def _(dve):
            nc.vector.memset(brow_in[:, :], 0.0).then_inc(brow_zeroed, 1)
            nc.vector.memset(sa_wide[:, :, :], 0.0).then_inc(sa_zeroed, 1)
            nc.vector.memset(w3[REST:P, FULL, :], 0.0).then_inc(w3_zeroed, 1)

            dve.wait_ge(sig_c_ready, 1)
            nc.vector.tensor_tensor(silu_c[:, :], c[:, :], sig_c[:, :], ALU.mult).then_inc(silu_ready, 1)

            def ln1_stats(h):
                dve.wait_ge(x_loaded[h], 16)
                for t in range(h * HT, (h + 1) * HT):
                    nc.vector.bn_stats(stats[:, t, :], x[:, t, :]).then_inc(stats_ready, 1)
                for t in range(h * HT, (h + 1) * HT):
                    dve.wait_ge(stats_ready, t + 1)
                    nc.vector.bn_aggr(meanvar[:, t, :], stats[:, t, :]).then_inc(aggr_ready, 1)
                dve.wait_ge(aggr_ready, (h + 1) * HT)
                nc.vector.tensor_scalar(var_eps[:, h * HT:(h + 1) * HT], meanvar[:, h * HT:(h + 1) * HT, 1],
                                        EPS, None, ALU.add).then_inc(var_ready, 1)

            def ln1_apply(h):
                dve.wait_ge(rstd_ready, h + 1)
                for t in range(h * HT, (h + 1) * HT):
                    nc.vector.tensor_scalar(xn[:, t, :], x[:, t, :], meanvar[:, t, 0:1], rstd[:, t:t + 1],
                                            ALU.subtract, ALU.mult).then_inc(xn_ready, 1)

            def split_w(n, k, cs):
                dve.wait_ge(w_hi_ready, n)
                nc.vector.scalar_tensor_tensor(w_lo[:, k, cs], w_in[:, k, cs], scale1[:, k:k + 1],
                                               w_hi[:, k, cs].bitcast(F32), ALU.mult, ALU.subtract
                                               ).then_inc(w_lo_ready, 1)

            def split_xt(h):
                for k in range(KC):
                    dve.wait_ge(t_hi_ready, KC * h + k + 1)
                    nc.vector.tensor_tensor(t_lo[:, k, cols(h)], xt_bank(h, k)[:, :],
                                            t_hi[:, k, cols(h)].bitcast(F32), ALU.subtract
                                            ).then_inc(t_lo_ready, 1)

            ln1_stats(0)
            dve.wait_ge(mod_a_summed, 1)
            nc.vector.tensor_scalar(scale1[:, :], misc[:, MOD0 + CA * KC:MOD0 + CA * KC + KC], 1.0, None,
                                    ALU.add).then_inc(mod_a_cols, 1)
            dve.wait_ge(sa_zeroed, 1)
            nc.vector.tensor_copy(sa_wide[:, :, 0:33:32],
                                  misc[:, MOD0:MOD0 + KC].unsqueeze(2).to_broadcast([P, KC, 2])
                                  ).then_inc(mod_a_cols, 1)
            nc.vector.tensor_copy(mod[:, SA, :], misc[:, MOD0:MOD0 + KC]).then_inc(mod_a_cols, 1)
            ln1_apply(0)
            dve.wait_ge(mod_a_cols, 3)
            for k in range(KC):
                split_w(k + 1, k, slice(0, 2 * D))
            ln1_stats(1)
            split_xt(0)
            dve.wait_ge(brow_loaded, 32)
            dve.wait_ge(brow_summed, 1)
            nc.vector.tensor_tensor(brow[:, :], bank[6][:, :], brow_in[:, :], ALU.add).then_inc(brow_ready, 1)
            ln1_apply(1)
            dve.wait_ge(brow_hi_ready, 1)
            dve.wait_ge(brow_ready, 1)
            nc.vector.tensor_tensor(brow_r[32:33, :], brow[32:33, :], brow_r[32:33, :].bitcast(F32), ALU.subtract
                                    ).then_inc(brow_lo_ready, 1)
            split_xt(1)
            for k in range(KC):
                split_w(KC + k + 1, k, slice(2 * D, 3 * D))

            dve.wait_ge(mod_b_summed, 1)
            nc.vector.tensor_copy(mod[:, GA:, :].rearrange("p v k -> p (v k)"),
                                  misc[:, MOD0 + GA * KC:MOD0 + 6 * KC]).then_inc(mod_b_cols, 1)
            nc.vector.tensor_scalar(scale2[:, :], misc[:, MOD0 + CB * KC:MOD0 + CB * KC + KC], 1.0, None,
                                    ALU.add).then_inc(mod_b_cols, 1)
            dve.wait_ge(mod_b_cols, 2)
            gates = mod[:, GA:GB + 1:GB - GA, :]
            nc.vector.tensor_scalar(gate_sign[:, :, :], gates, 0.0, 2.0, ALU.is_ge, ALU.mult).then_inc(gates_part, 1)
            nc.vector.tensor_scalar(gate_neg[:, :, :], gates, -1.0, MIN_GATE, ALU.mult, ALU.max).then_inc(gates_part, 1)
            dve.wait_ge(bcol_loaded, 32)
            nc.vector.tensor_tensor(shift_t[:, :], mod[:, SA, :], bo_in[:, :], ALU.add).then_inc(shift_ready, 1)
            dve.wait_ge(gates_part, 2)
            nc.vector.tensor_tensor(gate_size[:, :, :], gate_neg[:, :, :], gates, ALU.max).then_inc(gates_part, 1)
            dve.wait_ge(gates_part, 3)
            nc.vector.scalar_tensor_tensor(rows_src[:, 2:4, :], gate_sign[:, :, :], -1.0, gate_size[:, :, :],
                                           ALU.add, ALU.mult).then_inc(gates_ready, 1)
            dve.wait_ge(gates_ready, 1)
            dve.wait_ge(shift_ready, 1)
            nc.vector.tensor_tensor(rows_src[:, 0, :], rows_src[:, 2, :], scale1[:, :], ALU.mult
                                    ).then_inc(rows_src_ready, 1)
            nc.vector.tensor_tensor(rows_src[:, 1, :], rows_src[:, 2, :], shift_t[:, :], ALU.mult
                                    ).then_inc(rows_src_ready, 1)
            dve.wait_ge(bq_summed, 1)
            nc.vector.tensor_tensor(bq[:, :], misc[:, QB0:QB0 + KC], bq_in[:, :], ALU.add).then_inc(bq_ready, 1)

            def thresholds():
                dve.wait_ge(gamma_summed, 1)
                for dst, sign in ((thr, 1), (nthr, -1)):
                    nc.vector.tensor_scalar(dst[:, :], misc[:, G0:G0 + 3], sign * 0.5 / (HID * D),
                                            sign * 0.5 * QUANT_EPS, ALU.mult, ALU.add).then_inc(thr_ready, 1)

            def quantise(i):
                w = (w1, w2, w3)[i]
                dve.wait_ge(thr_ready, 2)
                if i > 0:
                    dve.wait_ge(quant_ready, i)
                n = w.shape[1] * w.shape[2]
                up = above[:, 0:n].rearrange("p (k n) -> p k n", n=w.shape[2])
                dst = (w12q[:, :, 0:HID], w12q[:, :, HID:], w3q[:, :, :])[i]
                nc.vector.tensor_scalar(up, w[:, :, :], nthr[:, i:i + 1], None, ALU.is_lt).then_inc(above_ready, 1)
                dve.wait_ge(above_ready, i + 1)
                nc.vector.scalar_tensor_tensor(dst, w[:, :, :], thr[:, i:i + 1], up, ALU.is_gt, ALU.subtract
                                               ).then_inc(quant_ready, 1)

            def rope_k(i):
                ts = slice(2 * i, 2 * i + 2)
                s = slice(2 * i % 4, 2 * i % 4 + 2)
                dve.wait_ge(kv_in_ready, 2 * i + 2)
                if i == 0:
                    dve.wait_ge(cosk_loaded, 16)
                    dve.wait_ge(sink_loaded, 16)
                if i >= 2:
                    dve.wait_ge(rope_k_ready, i - 1)
                kk = kv_in[:, ts, 0:ROT].rearrange("p t (a d) -> p t a d", a=2)
                nc.vector.tensor_tensor(kc[:, s, :, :], kk, cosk[:, ts, :].unsqueeze(2).to_broadcast([P, 2, 2, HALF]),
                                        ALU.mult).then_inc(rope_k_parts, 1)
                for e in range(2):
                    nc.vector.tensor_tensor(ks[:, s, e, :], kk[:, :, 1 - e, :], sink[:, ts, e, :], ALU.mult
                                            ).then_inc(rope_k_parts, 1)
                nc.vector.tensor_tensor(kv[:, ts, ROT:], kv_in[:, ts, ROT:D], kv_in[:, ts, D + ROT:], ALU.mult
                                        ).then_inc(kv_pass_ready, 1)

            def times_v(i):
                s = 2 * i % 4
                dve.wait_ge(rope_k_ready, i + 1)
                nc.vector.tensor_tensor(kv[:, 2 * i:2 * i + 2, 0:ROT],
                                        kr[:, s:s + 2, :, :].rearrange("p t a d -> p t (a d)"),
                                        kv_in[:, 2 * i:2 * i + 2, D:D + ROT], ALU.mult).then_inc(kv_rot_ready, 1)

            for i in range(TILES // 2):
                rope_k(i)
                if i > 0:
                    times_v(i - 1)
                if i in (1, 3):
                    g = i // 2
                    dve.wait_ge(squares_done, (g + 1) * HT)
                    nc.vector.tensor_scalar(ssq_min[:, g * HT:(g + 1) * HT], ssq[:, g * HT:(g + 1) * HT],
                                            MIN_NORM * MIN_NORM, None, ALU.max).then_inc(ssq_min_ready, 1)
            times_v(TILES // 2 - 1)
            thresholds()
            quantise(0)

            dve.wait_ge(ropeq_loaded, 32)
            dve.wait_ge(bq_ready, 1)
            for h in range(NH):
                dve.wait_ge(q_rot_done, h + 1)
                src = q_bank[h][0]
                nc.vector.scalar_tensor_tensor(qc[:, h, :], src[:, :], bq[:, 0:1], cosq[:, cols(h)],
                                               ALU.add, ALU.mult).then_inc(q_parts, 1)
                for a0, b0 in ((HALF, 0), (0, HALF)):
                    nc.vector.scalar_tensor_tensor(qs[b0:b0 + HALF, h, :], src[a0:a0 + HALF, :],
                                                   bq[a0:a0 + HALF, 0:1], sinq[a0:a0 + HALF, cols(h)],
                                                   ALU.add, ALU.mult).then_inc(q_parts, 1)

            dve.wait_ge(a_summed, 1)
            nc.vector.tensor_copy(a[:, :], misc[:, A0:A0 + KC]).then_inc(a_ready, 1)
            dve.wait_ge(a_ready, 1)
            dve.wait_ge(w_out_loaded, 16)
            dve.wait_ge(rows_ready, 2)
            for k in range(KC):
                nc.vector.scalar_tensor_tensor(wa[:, k, :], w_out[:, k, :], a[:, k:k + 1], rows[:, 2, :],
                                               ALU.mult, ALU.mult).then_inc(wa_ready, 1)
            quantise(1)

            def ln2_stats(h):
                for i in (2 * h, 2 * h + 1):
                    dve.wait_ge(y_done, i + 1)
                    dve.wait_ge(res_ready, h + 1)
                    pair = x1[:, 2 * i:2 * i + 2, :].rearrange("p t d -> p (t d)")
                    nc.vector.tensor_tensor(pair, y_bank[i][:, :], pair, ALU.add).then_inc(x1_ready, 1)
                    dve.wait_ge(x1_ready, i + 1)
                    for t in (2 * i, 2 * i + 1):
                        nc.vector.bn_stats(stats2[:, t, :], x1[:, t, :]).then_inc(stats2_ready, 1)
                for t in range(h * HT, (h + 1) * HT):
                    dve.wait_ge(stats2_ready, t + 1)
                    nc.vector.bn_aggr(meanvar2[:, t, :], stats2[:, t, :]).then_inc(aggr2_ready, 1)
                dve.wait_ge(aggr2_ready, (h + 1) * HT)
                nc.vector.tensor_scalar(var_eps2[:, h * HT:(h + 1) * HT], meanvar2[:, h * HT:(h + 1) * HT, 1],
                                        EPS, None, ALU.add).then_inc(var2_ready, 1)

            def ln2_apply(h):
                dve.wait_ge(rstd2_ready, h + 1)
                for t in range(h * HT, (h + 1) * HT):
                    nc.vector.tensor_scalar(xn[:, t, :], x1[:, t, :], meanvar2[:, t, 0:1], rstd2[:, t:t + 1],
                                            ALU.subtract, ALU.mult).then_inc(xn2_ready, 1)

            def split_h2(h):
                for k in range(KC):
                    n = KC * h + k + 1
                    dve.wait_ge(h2_ready, n)
                    nc.vector.tensor_copy(t_hi[:, k, cols(h)], h2[:, k, cols(h)]).then_inc(h2_hi_ready, 1)
                    dve.wait_ge(h2_hi_ready, n)
                    nc.vector.tensor_tensor(t_lo[:, k, cols(h)], h2[:, k, cols(h)],
                                            t_hi[:, k, cols(h)].bitcast(F32), ALU.subtract
                                            ).then_inc(h2_lo_ready, 1)

            ln2_stats(0)
            ln2_apply(0)
            ln2_stats(1)
            split_h2(0)
            ln2_apply(1)

            def product(n):
                h, j = ORDER[n]
                a_bank, b_bank = up_banks[n % 3]
                dve.wait_ge(sig_ready, n + 1)
                if n >= 3:
                    dve.wait_ge(hid_lo_ready, n - 2)
                    dve.wait_ge(hid_hi_ready, n - 2)
                if j < FULL:
                    nc.vector.tensor_tensor(hid[:, n % 3, :], b_bank[:, :], sig[:, n % 3, :], ALU.mult
                                            ).then_inc(hid_ready, 1)
                else:
                    nc.vector.tensor_tensor(hid[0:REST, n % 3, :], a_bank[REST:P, :], sig[0:REST, n % 3, :], ALU.mult
                                            ).then_inc(hid_ready, 1)

            def split_hid(n):
                h, j = ORDER[n]
                r = P if j < FULL else REST
                dve.wait_ge(hid_hi_ready, n + 1)
                nc.vector.tensor_tensor(hid_lo[0:r, j, cols(h)], hid[0:r, n % 3, :],
                                        hid_hi[0:r, j, cols(h)].bitcast(F32), ALU.subtract).then_inc(hid_lo_ready, 1)

            for n in range(len(ORDER)):
                product(n)
                if n == 0:
                    split_h2(1)
                if n == 2:
                    quantise(2)
                if n >= 1:
                    split_hid(n - 1)
            split_hid(len(ORDER) - 1)

            for i in range(TILES // 2):
                dve.wait_ge(down_done, i + 1)
                pair = x[:, 2 * i:2 * i + 2, :]
                nc.vector.tensor_tensor(pair, down_bank[i][:, :].rearrange("p (t d) -> p t d", t=2),
                                        rows[:, 3, :].unsqueeze(1).to_broadcast([P, 2, D]), ALU.mult
                                        ).then_inc(ffn_scaled, 1)
                dve.wait_ge(ffn_scaled, i + 1)
                nc.vector.tensor_tensor(pair, pair, x1[:, 2 * i:2 * i + 2, :], ALU.add).then_inc(out_ready, 1)

        @block.gpsimd
        def _(pool):
            nc.gpsimd.memset(minus_half[:, :], -0.5).then_inc(exponent_set, 1)
            nc.gpsimd.memset(ones[:, :], 1.0).then_inc(ones_set, 1)
            nc.gpsimd.memset(ones_r[:, :].bitcast(F32), 1.0).then_inc(ones_set, 1)
            pool.wait_ge(exponent_set, 1)
            for h in range(NH):
                pool.wait_ge(var_ready, h + 1)
                nc.gpsimd.tensor_tensor(rstd[:, h * HT:(h + 1) * HT], var_eps[:, h * HT:(h + 1) * HT],
                                        minus_half[:, 0:HT], ALU.pow).then_inc(rstd_ready, 1)
            def residual(h):
                ts = slice(h * HT, (h + 1) * HT)
                if h == 0:
                    pool.wait_ge(rows_ready, 1)
                pool.wait_ge(xn_ready, (h + 1) * HT)
                nc.gpsimd.tensor_tensor(x1[:, ts, :], xn[:, ts, :], rows[:, 0, :].unsqueeze(1).to_broadcast([P, HT, D]),
                                        ALU.mult).then_inc(res_scaled, 1)

            def residual_x(h):
                ts = slice(h * HT, (h + 1) * HT)
                pool.wait_ge(res_scaled, h + 1)
                nc.gpsimd.tensor_tensor(x1[:, ts, :], x1[:, ts, :], x[:, ts, :], ALU.add).then_inc(res_added, 1)

            def residual_g2(h):
                ts = slice(h * HT, (h + 1) * HT)
                pool.wait_ge(res_added, h + 1)
                nc.gpsimd.tensor_tensor(x1[:, ts, :], x1[:, ts, :], rows[:, 1, :].unsqueeze(1).to_broadcast([P, HT, D]),
                                        ALU.add).then_inc(res_ready, 1)

            def rope_k_sum(i):
                s = 2 * i % 4
                pool.wait_ge(rope_k_parts, 3 * (i + 1))
                if i >= 2:
                    pool.wait_ge(kv_rot_ready, i - 1)
                nc.gpsimd.tensor_tensor(kr[:, s:s + 2, :, :], kc[:, s:s + 2, :, :], ks[:, s:s + 2, :, :], ALU.add
                                        ).then_inc(rope_k_ready, 1)

            def norms(g):
                pool.wait_ge(ssq_min_ready, g + 1)
                nc.gpsimd.tensor_tensor(rnorm[:, g * HT:(g + 1) * HT], ssq_min[:, g * HT:(g + 1) * HT],
                                        minus_half[:, 0:HT], ALU.pow).then_inc(rnorm_ready, 1)

            for i in range(TILES // 2):
                rope_k_sum(i)
                if i == 0:
                    residual(0)
                if i == 1:
                    residual_x(0)
                    norms(0)
                if i == 2:
                    residual_g2(0)
            norms(1)
            for h in range(NH):
                pool.wait_ge(q_parts, 3 * (h + 1))
                nc.gpsimd.tensor_tensor(q[:, 0, cols(h)], qc[:, h, :], qs[:, h, :], ALU.add).then_inc(q_rot_ready, 1)
            residual(1)
            residual_x(1)
            residual_g2(1)
            for h in range(NH):
                pool.wait_ge(var2_ready, h + 1)
                nc.gpsimd.tensor_tensor(rstd2[:, h * HT:(h + 1) * HT], var_eps2[:, h * HT:(h + 1) * HT],
                                        minus_half[:, 0:HT], ALU.pow).then_inc(rstd2_ready, 1)
            pool.wait_ge(x1_ready, TILES // 2)
            pool.wait_ge(rstd2_ready, NH)
            for buf in (hid_hi, hid_lo):
                nc.gpsimd.memset(buf[REST:P, FULL, :].bitcast(F32), 0.0).then_inc(pads_zeroed, 1)

        @block.tensor
        def _(pe):
            def mod_columns(v0, v1):
                for m in range(v0 * KC, v1 * KC):
                    for k in range(KC):
                        last = nc.tensor.matmul(misc[:, MOD0 + m:MOD0 + m + 1], wm[:, k, m * P:(m + 1) * P],
                                                silu_c[:, k:k + 1], start=(k == 0), stop=(k == KC - 1))
                return last

            def turn(dst, src, h, done):
                for k in range(KC):
                    for t in range(HT):
                        last = nc.tensor.transpose(dst[k][:, t * P:(t + 1) * P],
                                                   src[:, h * HT + t, k * P:(k + 1) * P], ident[:, :])
                    last.then_inc(done, 1)

            pe.wait_ge(silu_ready, 1)
            pe.wait_ge(wm_a_loaded, 16)
            mod_columns(SA, GA).then_inc(mod_a_summed, 1)
            pe.wait_ge(ident_loaded, 16)
            pe.wait_ge(xn_ready, HT)
            turn([xt_bank(0, k) for k in range(KC)], xn, 0, xt_turned)
            pe.wait_ge(mod_a_cols, 3)
            pe.wait_ge(kv_w_loaded, 16)
            for k in range(KC):
                last = nc.tensor.matmul(bank[6][:, :], sa_wide[:, k, :], w_in[:, k, 0:2 * D],
                                        start=(k == 0), stop=(k == KC - 1))
            last.then_inc(brow_summed, 1)

            def kv_tile(t):
                h = t // HT
                if t >= 4:
                    pe.wait_ge(kv_in_ready, t - 3)
                pe.wait_ge(t_hi_ready, KC * (h + 1))
                pe.wait_ge(w_hi_ready, KC)
                tok = slice(t * P, (t + 1) * P)
                dst = kv_bank(t)[:, :]
                for k in range(KC):
                    nc.tensor.matmul(dst, t_hi[:, k, tok], w_hi[:, k, 0:2 * D], start=(k == 0), stop=False)
                pe.wait_ge(w_lo_ready, KC)
                for k in range(KC):
                    nc.tensor.matmul(dst, t_hi[:, k, tok], w_lo[:, k, 0:2 * D], start=False, stop=False)
                pe.wait_ge(t_lo_ready, KC * (h + 1))
                for k in range(KC):
                    nc.tensor.matmul(dst, t_lo[:, k, tok], w_hi[:, k, 0:2 * D], start=False, stop=False)
                pe.wait_ge(brow_lo_ready, 1)
                pe.wait_ge(ones_set, 2)
                nc.tensor.matmul(dst, ones_r[:, :], brow_r[:, :], start=False, stop=True).then_inc(kv_done, 1)

            pe.wait_ge(xn_ready, 2 * HT)
            turn([xt_bank(1, k) for k in range(KC)], xn, 1, xt_turned)
            kv_tile(0)
            pe.wait_ge(q_w_loaded, 16)
            for m in range(KC):
                for k in range(KC):
                    last = nc.tensor.matmul(misc[:, QB0 + m:QB0 + m + 1], w_in[:, k, 2 * D + m * P:2 * D + (m + 1) * P],
                                            mod[:, SA, k:k + 1], start=(k == 0), stop=(k == KC - 1))
            last.then_inc(bq_summed, 1)
            pe.wait_ge(wm_b_loaded, 16)
            mod_columns(GA, GB + 1).then_inc(mod_b_summed, 1)
            kv_tile(1)
            pe.wait_ge(rows_src_ready, 2)
            pe.wait_ge(t_lo_ready, 2 * KC)
            for i in range(2):
                for r in (2 * i, 2 * i + 1):
                    for k in range(KC):
                        at = (r % 2) * D + k * P
                        last = nc.tensor.transpose(bank[2 + i][:, at:at + P],
                                                   rows_src[:, r, k:k + 1].to_broadcast([P, P]), ident[:, :])
                last.then_inc(rows_spread, 1)

            for t in range(2, TILES):
                kv_tile(t)
            pe.wait_ge(abs_done, 3)
            pe.wait_ge(bq_ready, 1)
            nc.tensor.matmul(misc[:, G0:G0 + 3], ones[:, :], abs_sum[:, :], start=True, stop=True
                             ).then_inc(gamma_summed, 1)

            def q_part(h, m, done):
                cs = slice(2 * D + m * P, 2 * D + (m + 1) * P)
                terms = [(w_hi, t_hi), (w_hi, t_lo), (w_lo, t_hi)]
                for i, (w, t) in enumerate(terms):
                    for k in range(KC):
                        last = nc.tensor.matmul(q_bank[h][m][:, :], w[:, k, cs], t[:, k, cols(h)],
                                                start=(i == 0 and k == 0), stop=(i == 2 and k == KC - 1))
                last.then_inc(done, 1)

            pe.wait_ge(w_lo_ready, 2 * KC)
            pe.wait_ge(rows_ready, 2)
            q_part(0, 0, q_rot_done)
            pe.wait_ge(kv_in_ready, 6)
            q_part(1, 0, q_rot_done)
            q_part(0, 1, q_pass_done)
            q_part(1, 1, q_pass_done)

            pe.wait_ge(thr_ready, 2)
            pe.wait_ge(rnorm_ready, 2)
            pe.wait_ge(kv_rot_ready, TILES // 2)
            pe.wait_ge(kv_pass_ready, TILES // 2)
            for m in range(KC):
                for t in range(TILES):
                    last = nc.tensor.matmul(misc[:, A0 + m:A0 + m + 1], kv[:, t, m * P:(m + 1) * P], rnorm[:, t:t + 1],
                                            start=(t == 0), stop=(t == TILES - 1))
            last.then_inc(a_summed, 1)

            def y_tiles(i):
                h = i // 2
                if i % 2 == 0:
                    pe.wait_ge(q_rot_ready, h + 1)
                    pe.wait_ge(q_pass_ready, h + 1)
                if i == 3:
                    pe.wait_ge(q_parts, 3)
                for t in (2 * i, 2 * i + 1):
                    for k in range(KC):
                        last = nc.tensor.matmul(y_bank[i][:, (t % 2) * D:(t % 2 + 1) * D],
                                                q[:, k, t * P:(t + 1) * P], wa[:, k, :],
                                                start=(k == 0), stop=(k == KC - 1))
                last.then_inc(y_done, 1)

            pe.wait_ge(wa_ready, KC)
            for i in range(4):
                y_tiles(i)
            pe.wait_ge(xn2_ready, HT)
            turn(xt2_bank[0], xn, 0, xt2_turned)

            def up(n):
                h, j = ORDER[n]
                if n >= 3:
                    pe.wait_ge(hid_ready, n - 2)
                for m in range(2 if j < FULL else 1):
                    c0 = up_cols(j)[m]
                    dst = up_banks[n % 3][m]
                    for i, t in enumerate((t_hi, t_lo)):
                        for k in range(KC):
                            last = nc.tensor.matmul(dst[:, :], w12q[:, k, c0:c0 + P], t[:, k, cols(h)],
                                                    start=(i == 0 and k == 0), stop=(i == 1 and k == KC - 1))
                last.then_inc(up_done, 1)

            pe.wait_ge(quant_ready, 2)
            pe.wait_ge(h2_hi_ready, KC)
            pe.wait_ge(h2_lo_ready, KC)
            pe.wait_ge(x1_ready, 4)
            up(0)
            pe.wait_ge(xn2_ready, 2 * HT)
            turn(xt2_bank[1], xn, 1, xt2_turned)
            pe.wait_ge(h2_ready, KC)
            for n in range(1, len(ORDER)):
                if n == HC:
                    pe.wait_ge(h2_hi_ready, 2 * KC)
                    pe.wait_ge(h2_lo_ready, 2 * KC)
                up(n)

            pe.wait_ge(quant_ready, 3)
            pe.wait_ge(pads_zeroed, 2)
            pe.wait_ge(h2_ready, 2 * KC)
            for i in range(TILES // 2):
                h = i // 2
                if i >= 2:
                    pe.wait_ge(ffn_scaled, i - 1)
                for t in (2 * i, 2 * i + 1):
                    for j in range(HC):
                        pe.wait_ge(hid_hi_ready, HC * h + j + 1)
                        pe.wait_ge(hid_lo_ready, HC * h + j + 1)
                        for u in (hid_hi, hid_lo):
                            last = nc.tensor.matmul(down_bank[i][:, (t % 2) * D:(t % 2 + 1) * D],
                                                    u[:, j, t * P:(t + 1) * P], w3q[:, j, :],
                                                    start=(j == 0 and u is hid_hi), stop=(j == HC - 1 and u is hid_lo))
                last.then_inc(down_done, 1)


def rope_tables():
    inv_freq = (np.float32(1.0) / np.float32(10000.0) ** (np.arange(0, ROT, 2, dtype=np.float32) / np.float32(ROT)))
    freqs = np.arange(S, dtype=np.float32)[:, None] * inv_freq.astype(np.float32)[None, :]
    return np.cos(freqs).astype(np.float32), np.sin(freqs).astype(np.float32)


def kernel(**inputs):
    import concourse.bacc as bacc
    from concourse.bass_utils import run_bass_kernel_spmd

    g = {n: np.asarray(v) for n, v in inputs.items()}
    order = np.concatenate([np.arange(0, ROT, 2), np.arange(1, ROT, 2), np.arange(ROT, D)])
    rows_q, rows_k, rows_v = order, D + order, 2 * D + order
    kvq = np.concatenate([rows_k, rows_v, rows_q])
    cos, sin = rope_tables()
    token = np.arange(S).reshape(P, TILES).T.reshape(-1)
    hid2 = np.concatenate([np.arange(FULL * P, HID), np.arange(FULL * P)])
    arrays = {
        "x_in": g["L0_attn_X"][0],
        "w_in_t": g["L0_attn_W_in"][kvq].T,
        "b_in": g["L0_attn_b_in"][kvq][None, :],
        "b_q_cols": g["L0_attn_b_in"][rows_q].reshape(KC, P).T,
        "w_out_t": g["L0_attn_W_out"].T[order],
        "b_out_cols": g["L0_attn_b_out"].reshape(KC, P).T,
        "w1_t": g["L0_ffn_w1"].T,
        "w2_t": g["L0_ffn_w2"][hid2].T,
        "w3_t": g["L0_ffn_w3"].T,
        "c_cols": g["L0_c"].reshape(KC, P).T,
        "wmod": g["L0_wmod"],
        "cos_tok": cos,
        "sin_tok": np.concatenate([-sin, sin], axis=1),
        "cos_feat": np.concatenate([cos[token].T, cos[token].T], axis=0),
        "sin_feat": np.concatenate([sin[token].T, -sin[token].T], axis=0),
        "ident_in": np.eye(P, dtype=np.float32),
    }
    arrays = {n: np.ascontiguousarray(v) for n, v in arrays.items()}
    nc = bacc.Bacc("TRN2", target_bir_lowering=False, num_devices=1)
    args = [nc.dram_tensor(n, v.shape, mybir.dt.from_np(v.dtype), kind="ExternalInput").ap()
            for n, v in arrays.items()]
    out = nc.dram_tensor("out", (S, D), F32, kind="ExternalOutput").ap()
    adaln_block(nc, *args, out)
    r = run_bass_kernel_spmd(nc, [arrays], core_ids=[0])
    return np.asarray(r.results[0]["out"]).reshape(1, S, D)
```

```python
from contextlib import ExitStack

import numpy as np

import concourse.bass as bass
from concourse import mybir

F32 = mybir.dt.float32
F32R = mybir.dt.float32r
ALU = mybir.AluOpType
ACT = mybir.ActivationFunctionType

P = 128
S, D = 1024, 256
TILES = S // P
KC = D // P
ROT = D // 2
HALF = ROT // 2
HID = 704
FULL = HID // P
REST = HID - FULL * P
HC = FULL + 1
NH = 2
PAIRS = TILES // 2
N = S // NH
KEEP_WARM = 4
WARM_UP = 12
EPS = 1e-5
MIN_NORM = 1e-12
QUANT_EPS = 1e-8
MIN_GATE = 0.25
SA, CA, GA, SB, CB, GB = range(6)


def adaln_block(nc, x_in, w_in_t, b_in, b_q_cols, w_out_t, b_out_cols, w1_t, w2_t, w3_t, c_cols, wmod,
                cos_tok, sin_tok, cos_feat, sin_feat, ident_in, out):
    ctx = ExitStack()
    early = ExitStack()
    with ctx:
        def sb(name, shape, dt=F32):
            return ctx.enter_context(nc.sbuf_tensor(name, shape, dt))

        def early_sb(name, shape, dt=F32):
            return early.enter_context(nc.sbuf_tensor(name, shape, dt))

        def sem(name):
            return ctx.enter_context(nc.semaphore(name))

        x = sb("x", [P, TILES, D])
        w1 = sb("w1", [P, KC, HID])
        w2 = sb("w2", [P, KC, HID])
        w3 = sb("w3", [P, HC, D])
        c = sb("c", [P, KC])
        bq = sb("bq", [P, KC])
        bo = sb("bo", [P, KC])
        ident = sb("ident", [P, P])

        ones = sb("ones", [P, P])
        ones_r = sb("ones_r", [P, 2 * D], F32R)
        minus_half = sb("minus_half", [P, 2])

        sig_c = sb("sig_c", [P, KC])
        silu_c = sb("silu_c", [P, KC])
        mod = sb("mod", [P, 6, KC])
        scale1 = sb("scale1", [P, KC])
        scale2 = sb("scale2", [P, KC])
        gate_sign = sb("gate_sign", [P, 2, KC])
        gate_neg = sb("gate_neg", [P, 2, KC])
        gate_size = sb("gate_size", [P, 2, KC])
        rows_src = sb("rows_src", [P, 4, KC])
        shift = sb("shift", [P, KC])
        rows = sb("rows", [P, 4, D])

        stats = sb("stats", [P, 2, TILES, 6])
        meanvar = sb("meanvar", [P, 2, TILES, 2])
        var_eps = sb("var_eps", [P, 2, TILES])
        neg_mean = sb("neg_mean", [P, 2, TILES])
        rstd = sb("rstd", [P, 2, TILES])
        neg_mean_rstd = sb("neg_mean_rstd", [P, 2, TILES])
        xn = sb("xn", [P, TILES, D])
        x1 = sb("x1", [P, TILES, D])
        hm = sb("hm", [P, KC, S])
        hm_hi = sb("hm_hi", [P, KC, S], F32R)
        hm_lo = sb("hm_lo", [P, KC, S], F32R)

        abs_sum = sb("abs_sum", [P, 4])
        thr = sb("thr", [P, 3])
        nthr = sb("nthr", [P, 3])
        below_a, below_b = sb("below_a", [P, HC * D]), sb("below_b", [P, HC * D])
        w12q = sb("w12q", [P, KC, 2 * HID], F32R)
        w3q = sb("w3q", [P, HC, D], F32R)

        w_in = early_sb("w_in", [P, KC, 3 * D])
        w_hi = early_sb("w_hi", [P, KC, 3 * D], F32R)
        w_lo = early_sb("w_lo", [P, KC, 3 * D], F32R)
        w_out = early_sb("w_out", [P, KC, D])
        wm = early_sb("wm", [P, KC, 6 * D])
        cosk = early_sb("cosk", [P, TILES, HALF])
        sink = early_sb("sink", [P, TILES, 2, HALF])
        cosq = early_sb("cosq", [P, S])
        sinq = early_sb("sinq", [P, S])
        brow = early_sb("brow", [P, 2 * D])
        brow_r = early_sb("brow_r", [P, 2 * D], F32R)
        kv_in = early_sb("kv_in", [P, TILES, 2 * D])
        sq_junk = early_sb("sq_junk", [P, D])
        ssq = early_sb("ssq", [P, TILES])
        ssq_min = early_sb("ssq_min", [P, TILES])
        rnorm = early_sb("rnorm", [P, TILES])
        kc = early_sb("kc", [P, 4, 2, HALF])
        ks = early_sb("ks", [P, 4, 2, HALF])
        kr = early_sb("kr", [P, 4, 2, HALF])
        kv = early_sb("kv", [P, TILES, D])
        kv_sum = early_sb("kv_sum", [P, 2, D])
        a = early_sb("a", [P, KC])
        wa = early_sb("wa", [P, KC, D])
        qc = early_sb("qc", [P, 2, N])
        qs = early_sb("qs", [P, 2, N])
        q = early_sb("q", [P, KC, S])
        early.close()

        sig = sb("sig", [P, 3, N])
        hid = sb("hid", [P, 3, N])
        hid_hi = sb("hid_hi", [P, HC, S], F32R)
        hid_lo = sb("hid_lo", [P, FULL, S], F32R)

        bank = [ctx.enter_context(nc.psum_tensor(f"bank{i}", [P, 512], F32)) for i in range(8)]
        misc = bank[7]
        MOD0, G0, GB_ROW = 0, 32, D
        kv_bank = [bank[(4, 5, 0, 1)[t % 4]] for t in range(TILES)]
        q_bank = [(bank[2], bank[3]), (bank[4], bank[5])]
        y_bank = [bank[0], bank[1], bank[6], bank[2]]
        turn_bank = [[bank[i] for i in (0, 1, 2, 3)], [bank[i] for i in (3, 0, 1, 0)]]
        up_bank = [(bank[4], bank[5]), (bank[6], bank[7]), (bank[2], bank[3])]
        down_bank = [bank[i] for i in (0, 1, 4, 5, 6, 7, 2, 3)]

        x_loaded = [sem(f"x_loaded{i}") for i in range(3)]
        c_loaded, ident_loaded, bcol_loaded, brow_loaded = (
            sem("c_loaded"), sem("ident_loaded"), sem("bcol_loaded"), sem("brow_loaded"))
        wm_a_loaded, wm_ga_loaded, wm_b_loaded = sem("wm_a_loaded"), sem("wm_ga_loaded"), sem("wm_b_loaded")
        w_kv_loaded, w_q_loaded, w_out_loaded = sem("w_kv_loaded"), sem("w_q_loaded"), sem("w_out_loaded")
        ropek_loaded, ropeq_loaded = [sem("cosk_loaded"), sem("sink_loaded")], [sem("cosq_loaded"), sem("sinq_loaded")]
        ffn_loaded = [sem("w1_loaded"), sem("w2_loaded"), sem("w3_loaded")]
        out_stored = sem("out_stored")
        brow_zeroed, exponent_set, ones_set = sem("brow_zeroed"), sem("exponent_set"), sem("ones_set")
        sig_c_ready, silu_ready = sem("sig_c_ready"), sem("silu_ready")
        mod_summed, mod_a_ready, mod_ga_ready, mod_b_ready = (
            sem("mod_summed"), sem("mod_a_ready"), sem("mod_ga_ready"), sem("mod_b_ready"))
        gate_parts, gate_sized, gate_ready, shift_ready, rows_src_ready = (
            sem("gate_parts"), sem("gate_sized"), sem("gate_ready"), sem("shift_ready"), sem("rows_src_ready"))
        rows_spread, rows_ready = sem("rows_spread"), sem("rows_ready")
        stats_ready, aggr_ready, var_ready, rstd_ready, norm_ready = (
            sem("stats_ready"), sem("aggr_ready"), sem("var_ready"), sem("rstd_ready"), sem("norm_ready"))
        xn_ready, turned, hm_ready, hm_hi_ready, hm_lo_ready = (
            sem("xn_ready"), sem("turned"), sem("hm_ready"), sem("hm_hi_ready"), sem("hm_lo_ready"))
        w_hi_ready, w_lo_ready, brow_hi_ready, brow_lo_ready = (
            sem("w_hi_ready"), sem("w_lo_ready"), sem("brow_hi_ready"), sem("brow_lo_ready"))
        kv_done, kv_in_ready, squares_done = sem("kv_done"), sem("kv_in_ready"), sem("squares_done")
        rope_k_parts, rope_k_ready, kv_pass_ready, kv_rot_ready = (
            sem("rope_k_parts"), sem("rope_k_ready"), sem("kv_pass_ready"), sem("kv_rot_ready"))
        ssq_min_ready, rnorm_ready, kv_summed = sem("ssq_min_ready"), sem("rnorm_ready"), sem("kv_summed")
        a_summed, a_ready, wa_ready = sem("a_summed"), sem("a_ready"), sem("wa_ready")
        q_rot_done, q_pass_done, qc_ready, qs_ready, q_rot_ready, q_pass_ready = (
            sem("q_rot_done"), sem("q_pass_done"), sem("qc_ready"), sem("qs_ready"), sem("q_rot_ready"),
            sem("q_pass_ready"))
        res_scaled, res_added, res_ready, y_done, x1_ready = (
            sem("res_scaled"), sem("res_added"), sem("res_ready"), sem("y_done"), sem("x1_ready"))
        abs_done, gamma_summed, thr_ready, sign_ready = (
            sem("abs_done"), sem("gamma_summed"), sem("thr_ready"), sem("sign_ready"))
        w1_below_ready, w2_below_ready, w3_below_ready = (
            sem("w1_below_ready"), sem("w2_below_ready"), sem("w3_below_ready"))
        quant_ready = sem("quant_ready")
        up_done, sig_ready, hid_ready, hid_hi_ready, hid_lo_ready = (
            sem("up_done"), sem("sig_ready"), sem("hid_ready"), sem("hid_hi_ready"), sem("hid_lo_ready"))
        down_done, ffn_scaled, out_ready = sem("down_done"), sem("ffn_scaled"), sem("out_ready")

        ORDER = [(h, j) for h in range(NH) for j in range(HC)]

        def cols(h):
            return slice(h * N, (h + 1) * N)

        def pair_cols(i):
            return slice(2 * i * P, 2 * (i + 1) * P)

        def below(i):
            buf, (_, k, n) = (below_a, below_b, below_a)[i], (w1, w2, w3)[i].shape
            return buf[:, 0:k * n].rearrange("p (k n) -> p k n", n=n)

        def unit_rows(j):
            return slice(0, P if j < FULL else REST)

        block = ctx.enter_context(nc.Block())

        @block.sync
        def _(sp):
            xv = x_in.rearrange("(p t) d -> p t d", t=TILES)
            wv = w_in_t.rearrange("(k p) n -> p k n", p=P)
            wmv = wmod.rearrange("(k p) n -> p k n", p=P)
            sp.dma_start(x[:, 0:2, :], xv[:, 0:2, :]).then_inc(x_loaded[0], 16)
            sp.dma_start(wm[:, :, 0:GA * D], wmv[:, :, 0:GA * D]).then_inc(wm_a_loaded, 16)
            sp.dma_start(w_in[:, :, 0:2 * D], wv[:, :, 0:2 * D]).then_inc(w_kv_loaded, 16)
            sp.dma_start(x[:, 2:4, :], xv[:, 2:4, :]).then_inc(x_loaded[1], 16)
            sp.dma_start(x[:, 4:8, :], xv[:, 4:8, :]).then_inc(x_loaded[2], 16)
            sp.dma_start(wm[:, :, GA * D:SB * D], wmv[:, :, GA * D:SB * D]).then_inc(wm_ga_loaded, 16)
            sp.dma_start(w1[:, :, :], w1_t.rearrange("(k p) n -> p k n", p=P)).then_inc(ffn_loaded[0], 16)
            sp.dma_start(cosk[:, :, :], cos_tok.rearrange("(p t) d -> p t d", t=TILES)).then_inc(ropek_loaded[0], 16)
            sp.dma_start(sink[:, :, :, :], sin_tok.rearrange("(p t) (a d) -> p t a d", t=TILES, a=2)
                         ).then_inc(ropek_loaded[1], 16)
            sp.dma_start(w_in[:, :, 2 * D:], wv[:, :, 2 * D:]).then_inc(w_q_loaded, 16)
            sp.dma_start(w2[:, :, :], w2_t.rearrange("(k p) n -> p k n", p=P)).then_inc(ffn_loaded[1], 16)
            sp.dma_start(cosq[:, :], cos_feat).then_inc(ropeq_loaded[0], 16)
            sp.dma_start(sinq[:, :], sin_feat).then_inc(ropeq_loaded[1], 16)
            sp.dma_start(w_out[:, :, :], w_out_t.rearrange("(k p) n -> p k n", p=P)).then_inc(w_out_loaded, 16)
            sp.dma_start(wm[:, :, SB * D:], wmv[:, :, SB * D:]).then_inc(wm_b_loaded, 16)
            sp.dma_start(w3[:, 0:FULL, :], w3_t[0:FULL * P, :].rearrange("(k p) n -> p k n", p=P)
                         ).then_inc(ffn_loaded[2], 16)
            for r in (0, REST):
                sp.dma_start(w3[r:r + REST, FULL, :], w3_t[FULL * P:, :]).then_inc(ffn_loaded[2], 16)
            ov = out.rearrange("(p t) d -> p t d", t=TILES)
            stores = [(0, 2), (2, 4), (4, 6), (6, 7), (7, 8)]
            for t0, t1 in stores:
                sp.wait_ge(out_ready, t1)
                sp.dma_start(ov[:, t0:t1, :], x[:, t0:t1, :]).then_inc(out_stored, 16)
            sp.wait_ge(out_stored, 16 * len(stores))

        @block.scalar
        def _(act):
            act.dma_start(c[:, :], c_cols).then_inc(c_loaded, 16)
            act.dma_start(ident[:, :], ident_in).then_inc(ident_loaded, 16)
            nc.scalar.preload_act_table(ACT.Sigmoid)
            act.wait_ge(c_loaded, 16)
            nc.scalar.activation(sig_c[:, :], c[:, :], ACT.Sigmoid).then_inc(sig_c_ready, 1)
            act.wait_ge(brow_zeroed, 1)
            for r in (0, 32):
                act.dma_start(brow[r:r + 1, :], b_in[:, 0:2 * D]).then_inc(brow_loaded, 16)
            act.dma_start(bq[:, :], b_q_cols).then_inc(bcol_loaded, 16)
            act.dma_start(bo[:, :], b_out_cols).then_inc(bcol_loaded, 16)

            def modulate(layer, i):
                n = layer * PAIRS + i
                act.wait_ge(turned, n + 1)
                shift_c, scale_c = (SA, scale1) if layer == 0 else (SB, scale2)
                if layer == 1:
                    act.wait_ge(hm_lo_ready, PAIRS)
                for k in range(KC):
                    nc.scalar.activation(hm[:, k, pair_cols(i)], turn_bank[layer][i][:, k * 2 * P:(k + 1) * 2 * P],
                                         ACT.Identity, bias=mod[:, shift_c, k:k + 1], scale=scale_c[:, k:k + 1]
                                         ).then_inc(hm_ready, 1)

            def norm_apply(layer, i):
                src = (x, x1)[layer]
                act.wait_ge(norm_ready, layer * PAIRS + i + 1)
                if layer == 1:
                    act.wait_ge(res_scaled, i + 1)
                for t in (2 * i, 2 * i + 1):
                    nc.scalar.activation(xn[:, t, :], src[:, t, :], ACT.Identity, bias=neg_mean_rstd[:, layer, t:t + 1],
                                         scale=rstd[:, layer, t:t + 1]).then_inc(xn_ready, 1)

            act.wait_ge(w_kv_loaded, 16)
            nc.scalar.activation(w_hi[:, :, 0:2 * D], w_in[:, :, 0:2 * D], ACT.Identity).then_inc(w_hi_ready, 1)

            act.wait_ge(mod_a_ready, 2)
            modulate(0, 0)
            modulate(0, 1)
            act.wait_ge(brow_loaded, 32)
            nc.scalar.activation(brow_r[:, :], brow[:, :], ACT.Identity).then_inc(brow_hi_ready, 1)

            def spread_rows(i, src, r):
                act.wait_ge(rows_spread, i)
                nc.scalar.activation(rows[:, r, :], src, ACT.Identity).then_inc(rows_ready, 1)

            def abs_sums(i):
                act.wait_ge(ffn_loaded[i], 48 if i == 2 else 16)
                if i < 2:
                    parts = [(slice(0, P), slice(0, KC))]
                else:
                    act.wait_ge(w_lo_ready, 2)
                    parts = [(slice(0, P), slice(0, FULL)), (slice(0, REST), slice(FULL, HC))]
                for m, (rows_, chunks) in enumerate(parts):
                    magnitudes = below(i) if i < 2 else w_in[:, :, :].rearrange("p k (h n) -> p (k h) n", n=D)
                    nc.scalar.activation(magnitudes[rows_, chunks, :], (w1, w2, w3)[i][rows_, chunks, :], ACT.Abs,
                                         accum_out=abs_sum[rows_, i + m:i + m + 1]).then_inc(abs_done, 1)

            abs_sums(0)
            norm_apply(0, 2)
            norm_apply(0, 3)
            for t in range(TILES):
                act.wait_ge(kv_done, t + 1)
                nc.scalar.activation(kv_in[:, t, :], kv_bank[t][:, :], ACT.Identity).then_inc(kv_in_ready, 1)
                act.wait_ge(kv_in_ready, t + 1)
                if t > 0:
                    act.wait_ge(squares_done, t)
                nc.scalar.activation(sq_junk[:, :], kv_in[:, t, 0:D], ACT.Square,
                                     accum_out=ssq[:, t:t + 1]).then_inc(squares_done, 1)
                if t in (2, 3):
                    modulate(0, t)
                if t == 3:
                    for r in range(2):
                        spread_rows(1, bank[6][:, r * D:(r + 1) * D], r)
                if t == 6:
                    spread_rows(2, bank[3][:, 0:D], 2)
                if t == 3:
                    abs_sums(1)

            def q_pass(h):
                act.wait_ge(q_pass_done, h + 1)
                act.wait_ge(bcol_loaded, 32)
                nc.scalar.activation(q[:, 1, cols(h)], q_bank[h][1][:, :], ACT.Identity, bias=bq[:, 1:2]
                                     ).then_inc(q_pass_ready, 1)

            act.wait_ge(thr_ready, 4)
            act.wait_ge(abs_done, 2)
            nc.scalar.activation(below(1), w2[:, :, :], ACT.Sign, bias=nthr[:, 1:2], scale=-1.0).then_inc(sign_ready, 1)
            q_pass(0)
            act.wait_ge(sign_ready, 1)
            nc.scalar.activation(below(1), below(1), ACT.Relu).then_inc(w2_below_ready, 1)
            q_pass(1)
            abs_sums(2)

            norm_apply(1, 0)
            act.wait_ge(mod_b_ready, 2)
            modulate(1, 0)
            norm_apply(1, 1)
            modulate(1, 1)
            spread_rows(3, misc[:, GB_ROW:GB_ROW + D], 3)
            norm_apply(1, 2)
            norm_apply(1, 3)

            def hid_hi_part(n):
                h, j = ORDER[n]
                r = unit_rows(j)
                act.wait_ge(hid_ready, n + 1)
                nc.scalar.activation(hid_hi[r, j, cols(h)], hid[r, n % 3, :], ACT.Identity).then_inc(hid_hi_ready, 1)

            for n, (h, j) in enumerate(ORDER):
                r = unit_rows(j)
                act.wait_ge(up_done, n + 1)
                if n >= 3:
                    act.wait_ge(hid_ready, n - 2)
                nc.scalar.activation(sig[r, n % 3, :], up_bank[n % 3][0][r, :], ACT.Sigmoid).then_inc(sig_ready, 1)
                if n >= 1:
                    hid_hi_part(n - 1)
                if n in (2, 3):
                    modulate(1, n)
            hid_hi_part(len(ORDER) - 1)

        @block.vector
        def _(dve):
            nc.vector.memset(brow[:, :], 0.0).then_inc(brow_zeroed, 1)

            def norm_stats(layer, i):
                src = (x, x1)[layer]
                n = layer * TILES + 2 * i
                for t in (2 * i, 2 * i + 1):
                    nc.vector.bn_stats(stats[:, layer, t, :], src[:, t, :]).then_inc(stats_ready, 1)
                for m, t in enumerate((2 * i, 2 * i + 1)):
                    dve.wait_ge(stats_ready, n + m + 1)
                    nc.vector.bn_aggr(meanvar[:, layer, t, :], stats[:, layer, t, :]).then_inc(aggr_ready, 1)
                dve.wait_ge(aggr_ready, n + 2)
                nc.vector.tensor_scalar(var_eps[:, layer, 2 * i:2 * i + 2], meanvar[:, layer, 2 * i:2 * i + 2, 1],
                                        EPS, None, ALU.add).then_inc(var_ready, 1)
                nc.vector.tensor_scalar(neg_mean[:, layer, 2 * i:2 * i + 2], meanvar[:, layer, 2 * i:2 * i + 2, 0],
                                        -1.0, None, ALU.mult).then_inc(var_ready, 1)

            def norm_apply(i):
                dve.wait_ge(rstd_ready, i + 1)
                for t in (2 * i, 2 * i + 1):
                    nc.vector.tensor_scalar(xn[:, t, :], x[:, t, :], meanvar[:, 0, t, 0:1],
                                            rstd[:, 0, t:t + 1], ALU.subtract, ALU.mult).then_inc(xn_ready, 1)

            def split_hm(layer, i):
                n = layer * PAIRS + i + 1
                cs = pair_cols(i)
                dve.wait_ge(hm_ready, KC * n)
                nc.vector.tensor_copy(hm_hi[:, :, cs], hm[:, :, cs]).then_inc(hm_hi_ready, 1)
                dve.wait_ge(hm_hi_ready, n)
                nc.vector.tensor_tensor(hm_lo[:, :, cs], hm[:, :, cs], hm_hi[:, :, cs].bitcast(F32), ALU.subtract
                                        ).then_inc(hm_lo_ready, 1)

            def gate(n, v, r):
                g, s = mod[:, v, :], n
                nc.vector.tensor_scalar(gate_sign[:, s, :], g, 0.0, 2.0, ALU.is_ge, ALU.mult).then_inc(gate_parts, 1)
                nc.vector.tensor_scalar(gate_neg[:, s, :], g, -1.0, MIN_GATE, ALU.mult, ALU.max
                                        ).then_inc(gate_parts, 1)
                dve.wait_ge(gate_parts, 2 * n + 2)
                nc.vector.tensor_tensor(gate_size[:, s, :], gate_neg[:, s, :], g, ALU.max).then_inc(gate_sized, 1)
                dve.wait_ge(gate_sized, n + 1)
                nc.vector.scalar_tensor_tensor(rows_src[:, r, :], gate_sign[:, s, :], -1.0, gate_size[:, s, :],
                                               ALU.add, ALU.mult).then_inc(gate_ready, 1)

            def threshold(i):
                dve.wait_ge(gamma_summed, i + 1)
                for dst, sign in ((thr, 1), (nthr, -1)):
                    nc.vector.tensor_scalar(dst[:, i:i + 1], misc[:, G0 + i:G0 + i + 1], sign * 0.5 / (HID * D),
                                            sign * 0.5 * QUANT_EPS, ALU.mult, ALU.add).then_inc(thr_ready, 1)

            def misc_cols(v0, v1):
                return misc[:, MOD0 + v0 * KC:MOD0 + v1 * KC]

            dve.wait_ge(x_loaded[0], 16)
            norm_stats(0, 0)
            dve.wait_ge(sig_c_ready, 1)
            nc.vector.tensor_tensor(silu_c[:, :], c[:, :], sig_c[:, :], ALU.mult).then_inc(silu_ready, 1)
            norm_apply(0)
            dve.wait_ge(x_loaded[1], 16)
            norm_stats(0, 1)
            dve.wait_ge(mod_summed, 1)
            nc.vector.tensor_scalar(scale1[:, :], misc_cols(CA, GA), 1.0, None, ALU.add).then_inc(mod_a_ready, 1)
            nc.vector.tensor_copy(mod[:, SA, :], misc_cols(SA, CA)).then_inc(mod_a_ready, 1)
            norm_apply(1)
            split_hm(0, 0)
            split_hm(0, 1)
            dve.wait_ge(x_loaded[2], 16)
            norm_stats(0, 2)
            norm_stats(0, 3)

            threshold(0)
            dve.wait_ge(mod_summed, 2)
            nc.vector.tensor_copy(mod[:, GA, :], misc_cols(GA, SB)).then_inc(mod_ga_ready, 1)
            dve.wait_ge(bcol_loaded, 32)
            dve.wait_ge(mod_a_ready, 2)
            nc.vector.tensor_tensor(shift[:, :], mod[:, SA, :], bo[:, :], ALU.add).then_inc(shift_ready, 1)
            dve.wait_ge(mod_ga_ready, 1)
            gate(0, GA, 2)
            dve.wait_ge(gate_ready, 1)
            dve.wait_ge(shift_ready, 1)
            nc.vector.tensor_tensor(rows_src[:, 0, :], rows_src[:, 2, :], scale1[:, :], ALU.mult
                                    ).then_inc(rows_src_ready, 1)
            nc.vector.tensor_tensor(rows_src[:, 1, :], rows_src[:, 2, :], shift[:, :], ALU.mult
                                    ).then_inc(rows_src_ready, 1)

            def quantise(i, k0, k1):
                w = (w1, w2, w3)[i]
                dst = w3q[:, k0:k1, :] if i == 2 else w12q[:, k0:k1, i * HID:(i + 1) * HID]
                dve.wait_ge(thr_ready, 2 * i + 2)
                dve.wait_ge((w1_below_ready, w2_below_ready, w3_below_ready)[i], 1)
                nc.vector.scalar_tensor_tensor(dst, w[:, k0:k1, :], thr[:, i:i + 1], below(i)[:, k0:k1, :],
                                               ALU.is_gt, ALU.subtract).then_inc(quant_ready, 1)

            def rope_k(i):
                ts, s = slice(2 * i, 2 * i + 2), slice(2 * i % 4, 2 * i % 4 + 2)
                dve.wait_ge(kv_in_ready, 2 * i + 2)
                if i == 0:
                    dve.wait_ge(ropek_loaded[0], 16)
                    dve.wait_ge(ropek_loaded[1], 16)
                if i >= 2:
                    dve.wait_ge(rope_k_ready, i - 1)
                kk = kv_in[:, ts, 0:ROT].rearrange("p t (a d) -> p t a d", a=2)
                nc.vector.tensor_tensor(kc[:, s, :, :], kk, cosk[:, ts, :].unsqueeze(2).to_broadcast([P, 2, 2, HALF]),
                                        ALU.mult).then_inc(rope_k_parts, 1)
                for e in range(2):
                    nc.vector.tensor_tensor(ks[:, s, e, :], kk[:, :, 1 - e, :], sink[:, ts, e, :], ALU.mult
                                            ).then_inc(rope_k_parts, 1)
                nc.vector.tensor_tensor(kv[:, ts, ROT:], kv_in[:, ts, ROT:D], kv_in[:, ts, D + ROT:], ALU.mult
                                        ).then_inc(kv_pass_ready, 1)

            def norm_guard(i):
                dve.wait_ge(squares_done, 2 * i + 2)
                nc.vector.tensor_scalar(ssq_min[:, 2 * i:2 * i + 2], ssq[:, 2 * i:2 * i + 2], MIN_NORM * MIN_NORM,
                                        None, ALU.max).then_inc(ssq_min_ready, 1)

            def times_v(i):
                s = slice(2 * i % 4, 2 * i % 4 + 2)
                dve.wait_ge(rope_k_ready, i + 1)
                nc.vector.tensor_tensor(kv[:, 2 * i:2 * i + 2, 0:ROT],
                                        kr[:, s, :, :].rearrange("p t a d -> p t (a d)"),
                                        kv_in[:, 2 * i:2 * i + 2, D:D + ROT], ALU.mult).then_inc(kv_rot_ready, 1)

            def sum_kv(i):
                dve.wait_ge(kv_rot_ready, i + 1)
                dve.wait_ge(kv_pass_ready, i + 1)
                dve.wait_ge(rnorm_ready, i + 1)
                for e in range(2):
                    t = 2 * i + e
                    if i == 0:
                        nc.vector.tensor_scalar(kv_sum[:, e, :], kv[:, t, :], rnorm[:, t:t + 1], None, ALU.mult
                                                ).then_inc(kv_summed, 1)
                    else:
                        dve.wait_ge(kv_summed, t - 1)
                        nc.vector.scalar_tensor_tensor(kv_sum[:, e, :], kv[:, t, :], rnorm[:, t:t + 1],
                                                       kv_sum[:, e, :], ALU.mult, ALU.add).then_inc(kv_summed, 1)

            rope_k(0)
            norm_guard(0)
            dve.wait_ge(w_q_loaded, 16)
            nc.vector.tensor_copy(w_hi[:, :, 2 * D:], w_in[:, :, 2 * D:]).then_inc(w_hi_ready, 1)
            split_hm(0, 2)
            times_v(0)
            sum_kv(0)
            quantise(0, 0, 1)
            rope_k(1)
            norm_guard(1)
            split_hm(0, 3)
            times_v(1)
            sum_kv(1)
            quantise(0, 1, 2)
            rope_k(2)
            norm_guard(2)
            times_v(2)
            rope_k(3)
            norm_guard(3)
            threshold(1)
            sum_kv(2)

            def q_cos(h):
                dve.wait_ge(q_rot_done, h + 1)
                nc.vector.scalar_tensor_tensor(qc[:, h, :], q_bank[h][0][:, :], bq[:, 0:1], cosq[:, cols(h)],
                                               ALU.add, ALU.mult).then_inc(qc_ready, 1)

            def q_sin(h):
                for a0, b0 in ((HALF, 0), (0, HALF)):
                    nc.vector.scalar_tensor_tensor(qs[b0:b0 + HALF, h, :], q_bank[h][0][a0:a0 + HALF, :],
                                                   bq[a0:a0 + HALF, 0:1], sinq[a0:a0 + HALF, cols(h)],
                                                   ALU.add, ALU.mult).then_inc(qs_ready, 1)

            for r in ropeq_loaded:
                dve.wait_ge(r, 16)
            q_cos(0)
            times_v(3)
            sum_kv(3)
            q_sin(0)

            dve.wait_ge(a_summed, 1)
            nc.vector.tensor_copy(a[:, :], bank[6][:, 0:KC]).then_inc(a_ready, 1)
            dve.wait_ge(a_ready, 1)
            dve.wait_ge(w_out_loaded, 16)
            dve.wait_ge(rows_ready, 3)
            for k in range(KC):
                nc.vector.scalar_tensor_tensor(wa[:, k, :], w_out[:, k, :], a[:, k:k + 1], rows[:, 2, :],
                                               ALU.mult, ALU.mult).then_inc(wa_ready, 1)
            dve.wait_ge(mod_summed, 3)
            nc.vector.tensor_copy(mod[:, SB:, :].rearrange("p v k -> p (v k)"), misc_cols(SB, 6)
                                  ).then_inc(mod_b_ready, 1)
            nc.vector.tensor_scalar(scale2[:, :], misc_cols(CB, GB), 1.0, None, ALU.add).then_inc(mod_b_ready, 1)
            q_cos(1)
            q_sin(1)

            def add_y(i):
                dve.wait_ge(y_done, i + 1)
                dve.wait_ge(res_ready, i + 1)
                pair = x1[:, 2 * i:2 * i + 2, :].rearrange("p t d -> p (t d)")
                nc.vector.tensor_tensor(pair, y_bank[i][:, :], pair, ALU.add).then_inc(x1_ready, 1)
                dve.wait_ge(x1_ready, i + 1)

            add_y(0)
            norm_stats(1, 0)
            quantise(1, 0, 1)
            add_y(1)
            norm_stats(1, 1)
            dve.wait_ge(mod_b_ready, 1)
            gate(1, GB, 3)
            threshold(2)
            quantise(1, 1, 2)
            split_hm(1, 0)
            split_hm(1, 1)
            for i in (2, 3):
                add_y(i)
                norm_stats(1, i)

            def product(n):
                h, j = ORDER[n]
                first, second = up_bank[n % 3]
                r = unit_rows(j)
                dve.wait_ge(sig_ready, n + 1)
                if n >= 3:
                    dve.wait_ge(hid_lo_ready, n - 2)
                    dve.wait_ge(hid_hi_ready, n - 2)
                src = second[:, :] if j < FULL else first[REST:P, :]
                nc.vector.tensor_tensor(hid[r, n % 3, :], src, sig[r, n % 3, :], ALU.mult).then_inc(hid_ready, 1)

            def hid_lo_part(n):
                h, j = ORDER[n]
                r = unit_rows(j)
                dve.wait_ge(hid_hi_ready, n + 1)
                lo = hid_lo[:, j, cols(h)] if j < FULL else hid_hi[REST:P, FULL, cols(h)]
                nc.vector.tensor_tensor(lo, hid[r, n % 3, :], hid_hi[r, j, cols(h)].bitcast(F32),
                                        ALU.subtract).then_inc(hid_lo_ready, 1)

            for n in range(len(ORDER)):
                product(n)
                if n >= 1:
                    hid_lo_part(n - 1)
                if n in (2, 3):
                    split_hm(1, n)
                if n == 6:
                    quantise(2, 0, HC)
            hid_lo_part(len(ORDER) - 1)

            dve.wait_ge(rows_ready, 4)
            for t in range(TILES):
                dve.wait_ge(down_done, t + 1)
                nc.vector.tensor_tensor(x[:, t, :], down_bank[t][:, 0:D], rows[:, 3, :], ALU.mult
                                        ).then_inc(ffn_scaled, 1)
                dve.wait_ge(ffn_scaled, t + 1)
                nc.vector.tensor_tensor(x[:, t, :], x[:, t, :], x1[:, t, :], ALU.add).then_inc(out_ready, 1)

        @block.gpsimd
        def _(pool):
            nc.gpsimd.memset(minus_half[:, :], -0.5).then_inc(exponent_set, 1)
            nc.gpsimd.memset(ones[:, :], 1.0).then_inc(ones_set, 1)
            nc.gpsimd.memset(ones_r[:, :].bitcast(F32), 1.0).then_inc(ones_set, 1)

            def inv_std(layer, i):
                pool.wait_ge(var_ready, 2 * (layer * PAIRS + i + 1))
                pair = slice(2 * i, 2 * i + 2)
                nc.gpsimd.tensor_tensor(rstd[:, layer, pair], var_eps[:, layer, pair], minus_half[:, :], ALU.pow
                                        ).then_inc(rstd_ready, 1)
                pool.wait_ge(rstd_ready, layer * PAIRS + i + 1)
                nc.gpsimd.tensor_tensor(neg_mean_rstd[:, layer, pair], neg_mean[:, layer, pair], rstd[:, layer, pair],
                                        ALU.mult).then_inc(norm_ready, 1)

            pool.wait_ge(exponent_set, 1)
            inv_std(0, 0)
            inv_std(0, 1)

            def w_lo_part(n, cs):
                pool.wait_ge(w_hi_ready, n)
                nc.gpsimd.tensor_tensor(w_lo[:, :, cs], w_in[:, :, cs], w_hi[:, :, cs].bitcast(F32), ALU.subtract
                                        ).then_inc(w_lo_ready, 1)

            w_lo_part(1, slice(0, 2 * D))
            pool.wait_ge(brow_hi_ready, 1)
            pool.wait_ge(w_lo_ready, 1)
            nc.gpsimd.tensor_tensor(brow_r[32:33, :], brow[32:33, :], brow_r[32:33, :].bitcast(F32), ALU.subtract
                                    ).then_inc(brow_lo_ready, 1)
            pool.wait_ge(brow_lo_ready, 1)
            inv_std(0, 2)
            inv_std(0, 3)

            def residual(i, *steps):
                ts = slice(2 * i, 2 * i + 2)

                def row(r):
                    return rows[:, r, :].unsqueeze(1).to_broadcast([P, 2, D])

                if 0 in steps:
                    if i == 0:
                        pool.wait_ge(rows_ready, 2)
                    pool.wait_ge(xn_ready, 2 * i + 2)
                    nc.gpsimd.tensor_tensor(x1[:, ts, :], xn[:, ts, :], row(0), ALU.mult).then_inc(res_scaled, 1)
                if 1 in steps:
                    pool.wait_ge(res_scaled, i + 1)
                    nc.gpsimd.tensor_tensor(x1[:, ts, :], x1[:, ts, :], x[:, ts, :], ALU.add).then_inc(res_added, 1)
                if 2 in steps:
                    pool.wait_ge(res_added, i + 1)
                    nc.gpsimd.tensor_tensor(x1[:, ts, :], x1[:, ts, :], row(1), ALU.add).then_inc(res_ready, 1)

            def rope_k_sum(i):
                s = slice(2 * i % 4, 2 * i % 4 + 2)
                pool.wait_ge(rope_k_parts, 3 * (i + 1))
                if i >= 2:
                    pool.wait_ge(kv_rot_ready, i - 1)
                nc.gpsimd.tensor_tensor(kr[:, s, :, :], kc[:, s, :, :], ks[:, s, :, :], ALU.add).then_inc(rope_k_ready, 1)

            def inv_norm(i):
                pool.wait_ge(ssq_min_ready, i + 1)
                nc.gpsimd.tensor_tensor(rnorm[:, 2 * i:2 * i + 2], ssq_min[:, 2 * i:2 * i + 2],
                                        minus_half[:, :], ALU.pow).then_inc(rnorm_ready, 1)

            def q_sum(h):
                pool.wait_ge(qc_ready, h + 1)
                pool.wait_ge(qs_ready, 2 * (h + 1))
                nc.gpsimd.tensor_tensor(q[:, 0, cols(h)], qc[:, h, :], qs[:, h, :], ALU.add).then_inc(q_rot_ready, 1)

            def flags_below(i):
                pool.wait_ge(thr_ready, 2 * i + 2)
                nc.gpsimd.tensor_scalar(below(i), (w1, w2, w3)[i][:, :, :], nthr[:, i:i + 1], None, ALU.is_lt
                                        ).then_inc((w1_below_ready, w2_below_ready, w3_below_ready)[i], 1)

            pool.wait_ge(abs_done, 1)
            flags_below(0)
            rope_k_sum(0)
            inv_norm(0)
            w_lo_part(2, slice(2 * D, 3 * D))
            residual(0, 0)
            rope_k_sum(1)
            inv_norm(1)
            residual(0, 1)
            rope_k_sum(2)
            inv_norm(2)
            residual(0, 2)
            rope_k_sum(3)
            inv_norm(3)
            residual(1, 0, 1)
            q_sum(0)
            residual(1, 2)
            q_sum(1)
            residual(2, 0)
            inv_std(1, 0)
            residual(2, 1)
            inv_std(1, 1)
            residual(2, 2)
            residual(3, 0, 1, 2)
            inv_std(1, 2)
            inv_std(1, 3)
            pool.wait_ge(quant_ready, KC)
            flags_below(2)

        @block.tensor
        def _(pe):
            def mod_columns(v0, v1, signal=True):
                for m in range(v0 * KC, v1 * KC):
                    for k in range(KC):
                        last = nc.tensor.matmul(misc[:, MOD0 + m:MOD0 + m + 1], wm[:, k, m * P:(m + 1) * P],
                                                silu_c[:, k:k + 1], start=(k == 0), stop=(k == KC - 1))
                if signal:
                    last.then_inc(mod_summed, 1)

            def turn(layer, i, first=False):
                if first:
                    pe.wait_ge(ident_loaded, 16)
                pe.wait_ge(xn_ready, layer * TILES + 2 * i + 2)
                for k in range(KC):
                    for e in range(2):
                        at = (k * 2 + e) * P
                        last = nc.tensor.transpose(turn_bank[layer][i][:, at:at + P],
                                                   xn[:, 2 * i + e, k * P:(k + 1) * P], ident[:, :])
                last.then_inc(turned, 1)

            def kv_tiles(*tiles):
                def term(t, x_part, w_part, first=False):
                    for k in range(KC):
                        nc.tensor.matmul(kv_bank[t][:, :], x_part[:, k, t * P:(t + 1) * P], w_part[:, k, 0:2 * D],
                                         start=(first and k == 0), stop=False)

                for t in tiles:
                    if t in (2, 3):
                        pe.wait_ge(hm_ready, KC * (t - 1))
                    if t >= 4:
                        pe.wait_ge(kv_in_ready, t - 3)
                    pe.wait_ge(hm_hi_ready, t // 2 + 1)
                    pe.wait_ge(w_hi_ready, 1)
                    term(t, hm_hi, w_hi, first=True)
                for t in tiles:
                    pe.wait_ge(hm_lo_ready, t // 2 + 1)
                    term(t, hm_lo, w_hi)
                for t in tiles:
                    pe.wait_ge(w_lo_ready, 1)
                    term(t, hm_hi, w_lo)
                    pe.wait_ge(brow_lo_ready, 1)
                    nc.tensor.matmul(kv_bank[t][:, :], ones_r[:, 0:P], brow_r[:, :], start=False, stop=True
                                     ).then_inc(kv_done, 1)

            def spread(dst, r):
                for k in range(KC):
                    last = nc.tensor.transpose(dst[:, k * P:(k + 1) * P],
                                               rows_src[:, r, k:k + 1].to_broadcast([P, P]), ident[:, :])
                return last

            def gamma(i):
                pe.wait_ge(abs_done, i + 1)
                if i > 0:
                    pe.wait_ge(thr_ready, 2 * i)
                g = misc[:, G0 + i:G0 + i + 1]
                if i < 2:
                    nc.tensor.matmul(g, ones[:, :], abs_sum[:, i:i + 1], start=True, stop=True).then_inc(gamma_summed, 1)
                else:
                    pe.wait_ge(abs_done, 4)
                    nc.tensor.matmul(g, ones[:, :], abs_sum[:, 2:3], start=True, stop=False)
                    nc.tensor.matmul(g, ones[0:REST, :], abs_sum[0:REST, 3:4], start=False, stop=True
                                     ).then_inc(gamma_summed, 1)

            def keep_warm(dst, n):
                for _ in range(n):
                    nc.tensor.matmul(dst[:, :], ones_r[:, 0:P], ones_r[:, :], start=True, stop=True)

            pe.wait_ge(ones_set, 2)
            keep_warm(bank[6], WARM_UP)
            turn(0, 0, first=True)
            pe.wait_ge(silu_ready, 1)
            pe.wait_ge(wm_a_loaded, 16)
            mod_columns(SA, GA)
            turn(0, 1)
            keep_warm(bank[6], KEEP_WARM)
            kv_tiles(0, 1)
            pe.wait_ge(wm_ga_loaded, 16)
            pe.wait_ge(mod_a_ready, 2)
            mod_columns(GA, SB)
            gamma(0)
            turn(0, 2)
            kv_tiles(2)
            turn(0, 3)
            pe.wait_ge(rows_src_ready, 2)
            spread(bank[6][:, 0:D], 0)
            spread(bank[6][:, D:2 * D], 1).then_inc(rows_spread, 1)
            kv_tiles(3)
            kv_tiles(4)
            kv_tiles(5)
            pe.wait_ge(hm_ready, KC * PAIRS)
            spread(bank[3][:, 0:D], 2).then_inc(rows_spread, 1)
            kv_tiles(6)
            kv_tiles(7)
            gamma(1)

            def q_part(h, m, done):
                cs = slice(2 * D + m * P, 2 * D + (m + 1) * P)
                terms = [(w_hi, hm_hi), (w_hi, hm_lo), (w_lo, hm_hi)]
                for i, (w, t) in enumerate(terms):
                    if i == 2:
                        pe.wait_ge(w_lo_ready, 2)
                    for k in range(KC):
                        last = nc.tensor.matmul(q_bank[h][m][:, :], w[:, k, cs], t[:, k, cols(h)],
                                                start=(i == 0 and k == 0), stop=(i == 2 and k == KC - 1))
                last.then_inc(done, 1)

            pe.wait_ge(w_hi_ready, 2)
            q_part(0, 0, q_rot_done)
            pe.wait_ge(rows_ready, 3)
            q_part(0, 1, q_pass_done)
            pe.wait_ge(kv_in_ready, 6)
            pe.wait_ge(wm_b_loaded, 16)
            pe.wait_ge(thr_ready, 4)
            mod_columns(SB, GB, False)
            q_part(1, 0, q_rot_done)

            pe.wait_ge(kv_summed, TILES)
            pe.wait_ge(rows_ready, 2)
            for m in range(KC):
                for e in range(2):
                    last = nc.tensor.matmul(bank[6][:, m:m + 1], kv_sum[:, e, m * P:(m + 1) * P], ones[:, 0:1],
                                            start=(e == 0), stop=(e == 1))
            last.then_inc(a_summed, 1)
            mod_columns(GB, 6)
            q_part(1, 1, q_pass_done)

            def y_pair(i):
                if i < 2:
                    pe.wait_ge(kv_in_ready, TILES)
                if i == 3:
                    pe.wait_ge(qs_ready, 2)
                pe.wait_ge(q_rot_ready, i // 2 + 1)
                pe.wait_ge(q_pass_ready, i // 2 + 1)
                for e in range(2):
                    for k in range(KC):
                        t = 2 * i + e
                        last = nc.tensor.matmul(y_bank[i][:, e * D:(e + 1) * D], q[:, k, t * P:(t + 1) * P],
                                                wa[:, k, :], start=(k == 0), stop=(k == KC - 1))
                last.then_inc(y_done, 1)

            pe.wait_ge(wa_ready, KC)
            for i in range(3):
                y_pair(i)
            pe.wait_ge(mod_b_ready, 2)
            gamma(2)
            turn(1, 0)
            y_pair(3)
            pe.wait_ge(gate_ready, 2)
            pe.wait_ge(thr_ready, 6)
            spread(misc[:, GB_ROW:GB_ROW + D], 3).then_inc(rows_spread, 1)
            pe.wait_ge(x1_ready, 1)
            turn(1, 1)

            def up(n):
                h, j = ORDER[n]
                if n >= 3:
                    pe.wait_ge(hid_ready, n - 2)
                if n == 1:
                    pe.wait_ge(rows_ready, 4)
                    pe.wait_ge(x1_ready, 3)
                if n == 2:
                    pe.wait_ge(x1_ready, 4)
                    pe.wait_ge(hm_ready, KC * (PAIRS + 1))
                c0 = (j * P, (FULL + 1 + j) * P)
                for m in range(2 if j < FULL else 1):
                    for i, t in enumerate((hm_hi, hm_lo)):
                        for k in range(KC):
                            last = nc.tensor.matmul(up_bank[n % 3][m][:, :], w12q[:, k, c0[m]:c0[m] + P],
                                                    t[:, k, cols(h)], start=(i == 0 and k == 0),
                                                    stop=(i == 1 and k == KC - 1))
                last.then_inc(up_done, 1)

            pe.wait_ge(quant_ready, 2 * KC)
            pe.wait_ge(hm_hi_ready, PAIRS + 2)
            pe.wait_ge(hm_lo_ready, PAIRS + 2)
            pe.wait_ge(qs_ready, 4)
            up(0)
            for n in range(1, len(ORDER)):
                if n == 2:
                    pe.wait_ge(x1_ready, 2)
                    turn(1, 2)
                if n == 3:
                    pe.wait_ge(hm_ready, KC * (PAIRS + 2))
                    turn(1, 3)
                if n == HC:
                    pe.wait_ge(hm_hi_ready, 2 * PAIRS)
                    pe.wait_ge(hm_lo_ready, 2 * PAIRS)
                up(n)

            pe.wait_ge(quant_ready, 2 * KC + 1)
            pe.wait_ge(hm_ready, KC * 2 * PAIRS)
            for t in range(TILES):
                if t == 2:
                    pe.wait_ge(hid_ready, len(ORDER) - 2)
                if t == 4:
                    pe.wait_ge(hid_ready, len(ORDER) - 1)
                if t == 6:
                    pe.wait_ge(hid_ready, len(ORDER))
                for j in range(HC):
                    n = HC * (t // (TILES // NH)) + j + 1
                    pe.wait_ge(hid_hi_ready, n)
                    if j == FULL:
                        pe.wait_ge(hid_lo_ready, n)
                    last = nc.tensor.matmul(down_bank[t][:, 0:D], hid_hi[:, j, t * P:(t + 1) * P], w3q[:, j, :],
                                            start=(j == 0), stop=(j == FULL))
                    if j < FULL:
                        pe.wait_ge(hid_lo_ready, n)
                        nc.tensor.matmul(down_bank[t][:, 0:D], hid_lo[:, j, t * P:(t + 1) * P], w3q[:, j, :],
                                         start=False, stop=False)
                last.then_inc(down_done, 1)


def rope_tables():
    inv_freq = (np.float32(1.0) / np.float32(10000.0) ** (np.arange(0, ROT, 2, dtype=np.float32) / np.float32(ROT)))
    freqs = np.arange(S, dtype=np.float32)[:, None] * inv_freq.astype(np.float32)[None, :]
    return np.cos(freqs).astype(np.float32), np.sin(freqs).astype(np.float32)


def kernel(**inputs):
    import concourse.bacc as bacc
    from concourse.bass_utils import run_bass_kernel_spmd

    g = {n: np.asarray(v) for n, v in inputs.items()}
    order = np.concatenate([np.arange(0, ROT, 2), np.arange(1, ROT, 2), np.arange(ROT, D)])
    rows_q, rows_k, rows_v = order, D + order, 2 * D + order
    kvq = np.concatenate([rows_k, rows_v, rows_q])
    cos, sin = rope_tables()
    token = np.arange(S).reshape(P, TILES).T.reshape(-1)
    hid2 = np.concatenate([np.arange(FULL * P, HID), np.arange(FULL * P)])
    arrays = {
        "x_in": g["L0_attn_X"][0],
        "w_in_t": g["L0_attn_W_in"][kvq].T,
        "b_in": g["L0_attn_b_in"][kvq][None, :],
        "b_q_cols": g["L0_attn_b_in"][rows_q].reshape(KC, P).T,
        "w_out_t": g["L0_attn_W_out"].T[order],
        "b_out_cols": g["L0_attn_b_out"].reshape(KC, P).T,
        "w1_t": g["L0_ffn_w1"].T,
        "w2_t": g["L0_ffn_w2"][hid2].T,
        "w3_t": g["L0_ffn_w3"].T,
        "c_cols": g["L0_c"].reshape(KC, P).T,
        "wmod": g["L0_wmod"],
        "cos_tok": cos,
        "sin_tok": np.concatenate([-sin, sin], axis=1),
        "cos_feat": np.concatenate([cos[token].T, cos[token].T], axis=0),
        "sin_feat": np.concatenate([sin[token].T, -sin[token].T], axis=0),
        "ident_in": np.eye(P, dtype=np.float32),
    }
    arrays = {n: np.ascontiguousarray(v) for n, v in arrays.items()}
    nc = bacc.Bacc("TRN2", target_bir_lowering=False, num_devices=1)
    args = [nc.dram_tensor(n, v.shape, mybir.dt.from_np(v.dtype), kind="ExternalInput").ap()
            for n, v in arrays.items()]
    out = nc.dram_tensor("out", (S, D), F32, kind="ExternalOutput").ap()
    adaln_block(nc, *args, out)
    r = run_bass_kernel_spmd(nc, [arrays], core_ids=[0])
    return np.asarray(r.results[0]["out"]).reshape(1, S, D)
```

```python
from contextlib import ExitStack

import numpy as np

import concourse.bass as bass
from concourse import mybir

F32 = mybir.dt.float32
F32R = mybir.dt.float32r
ALU = mybir.AluOpType
ACT = mybir.ActivationFunctionType

P = 128
S, D = 1024, 256
TILES = S // P
KC = D // P
ROT = D // 2
HALF = ROT // 2
HID = 704
FULL = HID // P
REST = HID - FULL * P
HC = FULL + 1
NH = 2
PAIRS = TILES // 2
N = S // NH
WARM_UP = 11
KEEP_WARM = 4
EPS = 1e-5
MIN_NORM = 1e-12
QUANT_EPS = 1e-8
MIN_GATE = 0.25
SA, CA, GA, SB, CB, GB = range(6)


def adaln_block(nc, x_in, w_in_t, b_in, b_q_cols, w_out_t, b_out_cols, w1_t, w2_t, w3_t, c_cols, wmod,
                cos_tok, sin_tok, cos_feat, sin_feat, ident_in, out):
    ctx = ExitStack()
    early = ExitStack()
    with ctx:
        def sb(name, shape, dt=F32):
            return ctx.enter_context(nc.sbuf_tensor(name, shape, dt))

        def early_sb(name, shape, dt=F32):
            return early.enter_context(nc.sbuf_tensor(name, shape, dt))

        def sem(name):
            return ctx.enter_context(nc.semaphore(name))

        x = sb("x", [P, TILES, D])
        w1 = sb("w1", [P, KC, HID])
        w2 = sb("w2", [P, KC, HID])
        w3 = sb("w3", [P, HC, D])
        c = sb("c", [P, KC])
        bq = sb("bq", [P, KC])
        bo = sb("bo", [P, KC])
        ident = sb("ident", [P, P])

        ones = sb("ones", [P, P])
        ones_r = sb("ones_r", [P, 2 * D], F32R)
        minus_half = sb("minus_half", [P, 2])
        two_rows = sb("two_rows", [33, P], F32R)

        sig_c = sb("sig_c", [P, KC])
        silu_c = sb("silu_c", [P, KC])
        mod = sb("mod", [P, 6, KC])
        scale1 = sb("scale1", [P, KC])
        scale2 = sb("scale2", [P, KC])
        gate_sign = sb("gate_sign", [P, 2, KC])
        gate_neg = sb("gate_neg", [P, 2, KC])
        gate_size = sb("gate_size", [P, 2, KC])
        rows_src = sb("rows_src", [P, 4, KC])
        shift = sb("shift", [P, KC])
        rows = sb("rows", [P, 4, D])

        stats = sb("stats", [P, 2, TILES, 6])
        meanvar = sb("meanvar", [P, 2, TILES, 2])
        var_eps = sb("var_eps", [P, 2, TILES])
        neg_mean = sb("neg_mean", [P, 2, TILES])
        rstd = sb("rstd", [P, 2, TILES])
        neg_mean_rstd = sb("neg_mean_rstd", [P, 2, TILES])
        xn = sb("xn", [P, TILES, D])
        x1 = sb("x1", [P, TILES, D])
        hm = sb("hm", [P, KC, S])
        hm_hi = sb("hm_hi", [P, KC, S], F32R)
        hm_lo = sb("hm_lo", [P, KC, S], F32R)

        abs_sum = sb("abs_sum", [P, 4])
        thr = sb("thr", [P, 3])
        nthr = sb("nthr", [P, 3])
        below_a, below_b = sb("below_a", [P, HC * D]), sb("below_b", [P, HC * D])
        w12q = sb("w12q", [P, KC, 2 * HID], F32R)
        w3q = sb("w3q", [P, HC, D], F32R)

        w_in = early_sb("w_in", [P, KC, 3 * D])
        w_hi = early_sb("w_hi", [P, KC, 3 * D], F32R)
        w_lo = early_sb("w_lo", [P, KC, 3 * D], F32R)
        w_out = early_sb("w_out", [P, KC, D])
        wm = early_sb("wm", [P, KC, 6 * D])
        cosk = early_sb("cosk", [P, TILES, HALF])
        sink = early_sb("sink", [P, TILES, 2, HALF])
        cosq = early_sb("cosq", [P, S])
        sinq = early_sb("sinq", [P, S])
        brow = early_sb("brow", [P, 2 * D])
        brow_r = early_sb("brow_r", [P, 2 * D], F32R)
        kv_in = early_sb("kv_in", [P, TILES, 2 * D])
        sq_junk = early_sb("sq_junk", [P, D])
        ssq = early_sb("ssq", [P, TILES])
        ssq_min = early_sb("ssq_min", [P, TILES])
        rnorm = early_sb("rnorm", [P, TILES])
        kc = early_sb("kc", [P, 4, 2, HALF])
        ks = early_sb("ks", [P, 4, 2, HALF])
        kr = early_sb("kr", [P, 4, 2, HALF])
        kv = early_sb("kv", [P, TILES, D])
        kv_sum = early_sb("kv_sum", [P, 2, D])
        g2_r = early_sb("g2_r", [33, D], F32R)
        a = early_sb("a", [P, KC])
        wa = early_sb("wa", [P, KC, D])
        qc = early_sb("qc", [P, 2, N])
        qx = early_sb("qx", [P, 2, N])
        q = early_sb("q", [P, KC, S])
        early.close()

        sig = sb("sig", [P, 3, N])
        hid = sb("hid", [P, 3, N])
        hid_hi = sb("hid_hi", [P, HC, S], F32R)
        hid_lo = sb("hid_lo", [P, FULL, S], F32R)

        bank = [ctx.enter_context(nc.psum_tensor(f"bank{i}", [P, 512], F32)) for i in range(8)]
        misc = bank[7]
        MOD0, G0, GB_ROW = 0, 32, D
        kv_bank = [bank[(4, 5, 0, 1)[t % 4]] for t in range(TILES)]
        q_bank = [(bank[2], bank[3]), (bank[4], bank[5])]
        y_bank = [bank[0], bank[1], bank[6], bank[2]]
        turn_bank = [[bank[i] for i in (0, 1, 2, 3)], [bank[i] for i in (3, 0, 1, 0)]]
        up_bank = [(bank[4], bank[5]), (bank[6], bank[7]), (bank[2], bank[3])]
        down_bank = [bank[i] for i in (0, 1, 4, 5, 6, 7, 2, 3)]

        x_loaded = [sem(f"x_loaded{i}") for i in range(3)]
        c_loaded, ident_loaded, bcol_loaded, brow_loaded = (
            sem("c_loaded"), sem("ident_loaded"), sem("bcol_loaded"), sem("brow_loaded"))
        wm_a_loaded, wm_ga_loaded, wm_b_loaded = sem("wm_a_loaded"), sem("wm_ga_loaded"), sem("wm_b_loaded")
        w_kv_loaded, w_q_loaded, w_out_loaded = sem("w_kv_loaded"), sem("w_q_loaded"), sem("w_out_loaded")
        ropek_loaded, ropeq_loaded = [sem("cosk_loaded"), sem("sink_loaded")], [sem("cosq_loaded"), sem("sinq_loaded")]
        ffn_loaded = [sem("w1_loaded"), sem("w2_loaded"), sem("w3_loaded")]
        out_stored = sem("out_stored")
        g2_hi_ready, g2_lo_ready, selector_zeroed, selector_set = (
            sem("g2_hi_ready"), sem("g2_lo_ready"), sem("selector_zeroed"), sem("selector_set"))
        brow_zeroed, exponent_set, ones_set = sem("brow_zeroed"), sem("exponent_set"), sem("ones_set")
        sig_c_ready, silu_ready = sem("sig_c_ready"), sem("silu_ready")
        mod_summed, mod_a_ready, mod_ga_ready, mod_b_ready = (
            sem("mod_summed"), sem("mod_a_ready"), sem("mod_ga_ready"), sem("mod_b_ready"))
        gate_parts, gate_sized, gate_ready, shift_ready, rows_src_ready = (
            sem("gate_parts"), sem("gate_sized"), sem("gate_ready"), sem("shift_ready"), sem("rows_src_ready"))
        rows_spread, rows_ready = sem("rows_spread"), sem("rows_ready")
        stats_ready, aggr_ready, var_ready, rstd_ready, norm_ready = (
            sem("stats_ready"), sem("aggr_ready"), sem("var_ready"), sem("rstd_ready"), sem("norm_ready"))
        xn_ready, turned, hm_ready, hm_hi_ready, hm_lo_ready = (
            sem("xn_ready"), sem("turned"), sem("hm_ready"), sem("hm_hi_ready"), sem("hm_lo_ready"))
        hm_lo_pool_ready = sem("hm_lo_pool_ready")
        w_hi_ready, w_lo_ready, brow_hi_ready, brow_lo_ready = (
            sem("w_hi_ready"), sem("w_lo_ready"), sem("brow_hi_ready"), sem("brow_lo_ready"))
        kv_done, kv_in_ready, squares_done = sem("kv_done"), sem("kv_in_ready"), sem("squares_done")
        rope_k_parts, rope_k_ready, kv_pass_ready, kv_rot_ready = (
            sem("rope_k_parts"), sem("rope_k_ready"), sem("kv_pass_ready"), sem("kv_rot_ready"))
        kv_total_ready = sem("kv_total_ready")
        ssq_min_ready, rnorm_ready, kv_summed = sem("ssq_min_ready"), sem("rnorm_ready"), sem("kv_summed")
        a_summed, a_ready, wa_ready = sem("a_summed"), sem("a_ready"), sem("wa_ready")
        q_rot_done, q_pass_done, q_crossed, qc_ready, qs_ready, q_rot_ready, q_pass_ready = (
            sem("q_rot_done"), sem("q_pass_done"), sem("q_crossed"), sem("qc_ready"), sem("qs_ready"),
            sem("q_rot_ready"), sem("q_pass_ready"))
        res_scaled, res_ready, y_done, x1_ready = (
            sem("res_scaled"), sem("res_ready"), sem("y_done"), sem("x1_ready"))
        abs_done, gamma_summed, thr_ready, sign_ready = (
            sem("abs_done"), sem("gamma_summed"), sem("thr_ready"), sem("sign_ready"))
        w1_below_ready, w2_below_ready, w3_below_ready = (
            sem("w1_below_ready"), sem("w2_below_ready"), sem("w3_below_ready"))
        quant_ready = sem("quant_ready")
        up_done, sig_ready, hid_ready, hid_hi_ready, hid_lo_ready = (
            sem("up_done"), sem("sig_ready"), sem("hid_ready"), sem("hid_hi_ready"), sem("hid_lo_ready"))
        hid_lo0_ready = sem("hid_lo0_ready")
        down_done, ffn_scaled, out_ready = sem("down_done"), sem("ffn_scaled"), sem("out_ready")

        ORDER = [(h, j) for h in range(NH) for j in range(HC)]

        def cols(h):
            return slice(h * N, (h + 1) * N)

        def pair_cols(i):
            return slice(2 * i * P, 2 * (i + 1) * P)

        def below(i):
            buf, (_, k, n) = (below_a, below_b, below_a)[i], (w1, w2, w3)[i].shape
            return buf[:, 0:k * n].rearrange("p (k n) -> p k n", n=n)

        def unit_rows(j):
            return slice(0, P if j < FULL else REST)

        block = ctx.enter_context(nc.Block())

        @block.sync
        def _(sp):
            xv = x_in.rearrange("(p t) d -> p t d", t=TILES)
            wv = w_in_t.rearrange("(k p) n -> p k n", p=P)
            wmv = wmod.rearrange("(k p) n -> p k n", p=P)
            sp.dma_start(x[:, 0:2, :], xv[:, 0:2, :]).then_inc(x_loaded[0], 16)
            sp.dma_start(wm[:, :, 0:GA * D], wmv[:, :, 0:GA * D]).then_inc(wm_a_loaded, 16)
            sp.dma_start(x[:, 2:4, :], xv[:, 2:4, :]).then_inc(x_loaded[1], 16)
            sp.dma_start(w_in[:, :, 0:2 * D], wv[:, :, 0:2 * D]).then_inc(w_kv_loaded, 16)
            sp.dma_start(x[:, 4:8, :], xv[:, 4:8, :]).then_inc(x_loaded[2], 16)
            sp.dma_start(wm[:, :, GA * D:SB * D], wmv[:, :, GA * D:SB * D]).then_inc(wm_ga_loaded, 16)
            sp.dma_start(w1[:, :, :], w1_t.rearrange("(k p) n -> p k n", p=P)).then_inc(ffn_loaded[0], 16)
            sp.dma_start(cosk[:, :, :], cos_tok.rearrange("(p t) d -> p t d", t=TILES)).then_inc(ropek_loaded[0], 16)
            sp.dma_start(sink[:, :, :, :], sin_tok.rearrange("(p t) (a d) -> p t a d", t=TILES, a=2)
                         ).then_inc(ropek_loaded[1], 16)
            sp.dma_start(w_in[:, :, 2 * D:], wv[:, :, 2 * D:]).then_inc(w_q_loaded, 16)
            sp.dma_start(w2[:, :, :], w2_t.rearrange("(k p) n -> p k n", p=P)).then_inc(ffn_loaded[1], 16)
            sp.dma_start(wm[:, :, SB * D:], wmv[:, :, SB * D:]).then_inc(wm_b_loaded, 16)
            sp.dma_start(cosq[:, :], cos_feat).then_inc(ropeq_loaded[0], 16)
            sp.dma_start(sinq[:, :], sin_feat).then_inc(ropeq_loaded[1], 16)
            sp.dma_start(w_out[:, :, :], w_out_t.rearrange("(k p) n -> p k n", p=P)).then_inc(w_out_loaded, 16)
            sp.dma_start(w3[:, 0:FULL, :], w3_t[0:FULL * P, :].rearrange("(k p) n -> p k n", p=P)
                         ).then_inc(ffn_loaded[2], 16)
            for r in (0, REST):
                sp.dma_start(w3[r:r + REST, FULL, :], w3_t[FULL * P:, :]).then_inc(ffn_loaded[2], 16)
            ov = out.rearrange("(p t) d -> p t d", t=TILES)
            stores = [(0, 2), (2, 4), (4, 6), (6, 7), (7, 8)]
            for t0, t1 in stores:
                sp.wait_ge(out_ready, t1)
                sp.dma_start(ov[:, t0:t1, :], x[:, t0:t1, :]).then_inc(out_stored, 16)
            sp.wait_ge(out_stored, 16 * len(stores))

        @block.scalar
        def _(act):
            act.dma_start(c[:, :], c_cols).then_inc(c_loaded, 16)
            act.dma_start(ident[:, :], ident_in).then_inc(ident_loaded, 16)
            nc.scalar.preload_act_table(ACT.Sigmoid)
            act.wait_ge(c_loaded, 16)
            nc.scalar.activation(sig_c[:, :], c[:, :], ACT.Sigmoid).then_inc(sig_c_ready, 1)
            act.wait_ge(brow_zeroed, 1)
            for r in (0, 32):
                act.dma_start(brow[r:r + 1, :], b_in[:, 0:2 * D]).then_inc(brow_loaded, 16)
            act.dma_start(bq[:, :], b_q_cols).then_inc(bcol_loaded, 16)
            act.dma_start(bo[:, :], b_out_cols).then_inc(bcol_loaded, 16)

            def modulate(layer, i):
                n = layer * PAIRS + i
                act.wait_ge(turned, n + 1)
                shift_c, scale_c = (SA, scale1) if layer == 0 else (SB, scale2)
                if layer == 1:
                    act.wait_ge(hm_lo_ready, PAIRS)
                for k in range(KC):
                    nc.scalar.activation(hm[:, k, pair_cols(i)], turn_bank[layer][i][:, k * 2 * P:(k + 1) * 2 * P],
                                         ACT.Identity, bias=mod[:, shift_c, k:k + 1], scale=scale_c[:, k:k + 1]
                                         ).then_inc(hm_ready, 1)

            def norm_apply(layer, i):
                src = (x, x1)[layer]
                act.wait_ge(norm_ready, layer * PAIRS + i + 1)
                if layer == 1:
                    act.wait_ge(res_scaled, i + 1)
                    act.wait_ge(xn_ready, TILES + 2 * i)
                for t in (2 * i, 2 * i + 1):
                    nc.scalar.activation(xn[:, t, :], src[:, t, :], ACT.Identity, bias=neg_mean_rstd[:, layer, t:t + 1],
                                         scale=rstd[:, layer, t:t + 1]).then_inc(xn_ready, 1)

            act.wait_ge(w_kv_loaded, 16)
            nc.scalar.activation(w_hi[:, :, 0:2 * D], w_in[:, :, 0:2 * D], ACT.Identity).then_inc(w_hi_ready, 1)

            act.wait_ge(mod_a_ready, 2)
            modulate(0, 0)
            act.wait_ge(brow_loaded, 32)
            nc.scalar.activation(brow_r[:, :], brow[:, :], ACT.Identity).then_inc(brow_hi_ready, 1)
            modulate(0, 1)

            def spread_rows(i, src, r):
                act.wait_ge(rows_spread, i)
                nc.scalar.activation(rows[:, r, :], src, ACT.Identity).then_inc(rows_ready, 1)

            def abs_sums(i):
                act.wait_ge(ffn_loaded[i], 48 if i == 2 else 16)
                if i < 2:
                    parts = [(slice(0, P), slice(0, KC))]
                else:
                    act.wait_ge(w_lo_ready, 2)
                    parts = [(slice(0, P), slice(0, FULL)), (slice(0, REST), slice(FULL, HC))]
                for m, (rows_, chunks) in enumerate(parts):
                    magnitudes = below(i) if i < 2 else w_in[:, :, :].rearrange("p k (h n) -> p (k h) n", n=D)
                    nc.scalar.activation(magnitudes[rows_, chunks, :], (w1, w2, w3)[i][rows_, chunks, :], ACT.Abs,
                                         accum_out=abs_sum[rows_, i + m:i + m + 1]).then_inc(abs_done, 1)

            abs_sums(0)
            norm_apply(0, 2)
            norm_apply(0, 3)
            modulate(0, 2)
            for t in range(TILES):
                act.wait_ge(kv_done, t + 1)
                nc.scalar.activation(kv_in[:, t, :], kv_bank[t][:, :], ACT.Identity).then_inc(kv_in_ready, 1)
                act.wait_ge(kv_in_ready, t + 1)
                if t > 0:
                    act.wait_ge(squares_done, t)
                nc.scalar.activation(sq_junk[:, :], kv_in[:, t, 0:D], ACT.Square,
                                     accum_out=ssq[:, t:t + 1]).then_inc(squares_done, 1)
                if t == 1:
                    modulate(0, 3)
                if t == 3:
                    for r in range(2):
                        spread_rows(1, bank[6][:, r * D:(r + 1) * D], r)
                    nc.scalar.activation(g2_r[:, :], bank[6][0:33, D:2 * D], ACT.Identity).then_inc(g2_hi_ready, 1)
                if t == 4:
                    spread_rows(2, bank[3][:, 0:D], 2)
                if t == 5:
                    abs_sums(1)

            def q_pass(h):
                act.wait_ge(q_pass_done, h + 1)
                act.wait_ge(bcol_loaded, 32)
                nc.scalar.activation(q[:, 1, cols(h)], q_bank[h][1][:, :], ACT.Identity, bias=bq[:, 1:2]
                                     ).then_inc(q_pass_ready, 1)

            def q_cross(h):
                act.wait_ge(q_rot_done, h + 1)
                act.wait_ge(bcol_loaded, 32)
                for a0, b0 in ((HALF, 0), (0, HALF)):
                    nc.scalar.activation(qx[b0:b0 + HALF, h, :], q_bank[h][0][a0:a0 + HALF, :], ACT.Identity,
                                         bias=bq[a0:a0 + HALF, 0:1]).then_inc(q_crossed, 1)

            q_cross(0)
            act.wait_ge(thr_ready, 4)
            act.wait_ge(abs_done, 2)
            nc.scalar.activation(below(1), w2[:, :, :], ACT.Sign, bias=nthr[:, 1:2], scale=-1.0).then_inc(sign_ready, 1)
            act.wait_ge(sign_ready, 1)
            nc.scalar.activation(below(1), below(1), ACT.Relu).then_inc(w2_below_ready, 1)
            q_pass(0)
            q_cross(1)
            q_pass(1)
            spread_rows(3, misc[:, GB_ROW:GB_ROW + D], 3)
            abs_sums(2)

            norm_apply(1, 0)
            act.wait_ge(mod_b_ready, 3)
            modulate(1, 0)
            modulate(1, 1)

            def hid_hi_part(n):
                h, j = ORDER[n]
                r = unit_rows(j)
                act.wait_ge(hid_ready, n + 1)
                nc.scalar.activation(hid_hi[r, j, cols(h)], hid[r, n % 3, :], ACT.Identity).then_inc(hid_hi_ready, 1)

            for n, (h, j) in enumerate(ORDER):
                r = unit_rows(j)
                act.wait_ge(up_done, n + 1)
                if n >= 3:
                    act.wait_ge(hid_ready, n - 2)
                nc.scalar.activation(sig[r, n % 3, :], up_bank[n % 3][0][r, :], ACT.Sigmoid).then_inc(sig_ready, 1)
                if n == 0:
                    norm_apply(1, 2)
                if n == 3:
                    modulate(1, 3)
                if n >= 1:
                    hid_hi_part(n - 1)
                if n == 1:
                    modulate(1, 2)
            hid_hi_part(len(ORDER) - 1)

        @block.vector
        def _(dve):
            nc.vector.memset(brow[:, :], 0.0).then_inc(brow_zeroed, 1)
            nc.vector.memset(two_rows[:, :].bitcast(F32), 0.0).then_inc(selector_zeroed, 1)
            dve.wait_ge(selector_zeroed, 1)
            for r in (0, 32):
                nc.vector.memset(two_rows[r:r + 1, :].bitcast(F32), 1.0).then_inc(selector_set, 1)

            def norm_stats(layer, i):
                src = (x, x1)[layer]
                n = layer * TILES + 2 * i
                for t in (2 * i, 2 * i + 1):
                    nc.vector.bn_stats(stats[:, layer, t, :], src[:, t, :]).then_inc(stats_ready, 1)
                for m, t in enumerate((2 * i, 2 * i + 1)):
                    dve.wait_ge(stats_ready, n + m + 1)
                    nc.vector.bn_aggr(meanvar[:, layer, t, :], stats[:, layer, t, :]).then_inc(aggr_ready, 1)
                dve.wait_ge(aggr_ready, n + 2)
                nc.vector.tensor_scalar(var_eps[:, layer, 2 * i:2 * i + 2], meanvar[:, layer, 2 * i:2 * i + 2, 1],
                                        EPS, None, ALU.add).then_inc(var_ready, 1)
                nc.vector.tensor_scalar(neg_mean[:, layer, 2 * i:2 * i + 2], meanvar[:, layer, 2 * i:2 * i + 2, 0],
                                        -1.0, None, ALU.mult).then_inc(var_ready, 1)

            def norm_apply(layer, i):
                dve.wait_ge(rstd_ready, layer * PAIRS + i + 1)
                if layer == 1:
                    dve.wait_ge(res_scaled, i + 1)
                    dve.wait_ge(xn_ready, TILES + 2 * i)
                for t in (2 * i, 2 * i + 1):
                    nc.vector.tensor_scalar(xn[:, t, :], (x, x1)[layer][:, t, :], meanvar[:, layer, t, 0:1],
                                            rstd[:, layer, t:t + 1], ALU.subtract, ALU.mult).then_inc(xn_ready, 1)

            def split_hm(layer, i):
                n = layer * PAIRS + i + 1
                cs = pair_cols(i)
                dve.wait_ge(hm_ready, KC * n)
                nc.vector.tensor_copy(hm_hi[:, :, cs], hm[:, :, cs]).then_inc(hm_hi_ready, 1)
                if n == PAIRS + 3:
                    return
                dve.wait_ge(hm_hi_ready, n)
                nc.vector.tensor_tensor(hm_lo[:, :, cs], hm[:, :, cs], hm_hi[:, :, cs].bitcast(F32), ALU.subtract
                                        ).then_inc(hm_lo_ready, 1)

            def gate(n, v, r):
                g, s = mod[:, v, :], n
                nc.vector.tensor_scalar(gate_sign[:, s, :], g, 0.0, 2.0, ALU.is_ge, ALU.mult).then_inc(gate_parts, 1)
                nc.vector.tensor_scalar(gate_neg[:, s, :], g, -1.0, MIN_GATE, ALU.mult, ALU.max
                                        ).then_inc(gate_parts, 1)
                dve.wait_ge(gate_parts, 2 * n + 2)
                nc.vector.tensor_tensor(gate_size[:, s, :], gate_neg[:, s, :], g, ALU.max).then_inc(gate_sized, 1)
                dve.wait_ge(gate_sized, n + 1)
                nc.vector.scalar_tensor_tensor(rows_src[:, r, :], gate_sign[:, s, :], -1.0, gate_size[:, s, :],
                                               ALU.add, ALU.mult).then_inc(gate_ready, 1)

            def threshold(i):
                dve.wait_ge(gamma_summed, i + 1)
                for dst, sign in ((thr, 1), (nthr, -1)):
                    nc.vector.tensor_scalar(dst[:, i:i + 1], misc[:, G0 + i:G0 + i + 1], sign * 0.5 / (HID * D),
                                            sign * 0.5 * QUANT_EPS, ALU.mult, ALU.add).then_inc(thr_ready, 1)

            def misc_cols(v0, v1):
                return misc[:, MOD0 + v0 * KC:MOD0 + v1 * KC]

            dve.wait_ge(x_loaded[0], 16)
            norm_stats(0, 0)
            dve.wait_ge(sig_c_ready, 1)
            nc.vector.tensor_tensor(silu_c[:, :], c[:, :], sig_c[:, :], ALU.mult).then_inc(silu_ready, 1)
            norm_apply(0, 0)
            dve.wait_ge(x_loaded[1], 16)
            norm_stats(0, 1)
            dve.wait_ge(mod_summed, 1)
            nc.vector.tensor_scalar(scale1[:, :], misc_cols(CA, GA), 1.0, None, ALU.add).then_inc(mod_a_ready, 1)
            nc.vector.tensor_copy(mod[:, SA, :], misc_cols(SA, CA)).then_inc(mod_a_ready, 1)
            norm_apply(0, 1)
            split_hm(0, 0)
            dve.wait_ge(x_loaded[2], 16)
            norm_stats(0, 2)
            split_hm(0, 1)
            norm_stats(0, 3)

            threshold(0)
            dve.wait_ge(mod_summed, 2)
            nc.vector.tensor_copy(mod[:, GA, :], misc_cols(GA, SB)).then_inc(mod_ga_ready, 1)
            dve.wait_ge(bcol_loaded, 32)
            dve.wait_ge(mod_a_ready, 2)
            nc.vector.tensor_tensor(shift[:, :], mod[:, SA, :], bo[:, :], ALU.add).then_inc(shift_ready, 1)
            dve.wait_ge(mod_ga_ready, 1)
            gate(0, GA, 2)
            dve.wait_ge(gate_ready, 1)
            dve.wait_ge(shift_ready, 1)
            nc.vector.tensor_tensor(rows_src[:, 0, :], rows_src[:, 2, :], scale1[:, :], ALU.mult
                                    ).then_inc(rows_src_ready, 1)
            nc.vector.tensor_tensor(rows_src[:, 1, :], rows_src[:, 2, :], shift[:, :], ALU.mult
                                    ).then_inc(rows_src_ready, 1)

            def quantise(i, k0, k1):
                w = (w1, w2, w3)[i]
                dst = w3q[:, k0:k1, :] if i == 2 else w12q[:, k0:k1, i * HID:(i + 1) * HID]
                dve.wait_ge(thr_ready, 2 * i + 2)
                dve.wait_ge((w1_below_ready, w2_below_ready, w3_below_ready)[i], 1)
                nc.vector.scalar_tensor_tensor(dst, w[:, k0:k1, :], thr[:, i:i + 1], below(i)[:, k0:k1, :],
                                               ALU.is_gt, ALU.subtract).then_inc(quant_ready, 1)

            def rope_k(i):
                ts, s = slice(2 * i, 2 * i + 2), slice(2 * i % 4, 2 * i % 4 + 2)
                dve.wait_ge(kv_in_ready, 2 * i + 2)
                if i == 0:
                    dve.wait_ge(ropek_loaded[0], 16)
                    dve.wait_ge(ropek_loaded[1], 16)
                if i >= 2:
                    dve.wait_ge(rope_k_ready, i - 1)
                kk = kv_in[:, ts, 0:ROT].rearrange("p t (a d) -> p t a d", a=2)
                nc.vector.tensor_tensor(kc[:, s, :, :], kk, cosk[:, ts, :].unsqueeze(2).to_broadcast([P, 2, 2, HALF]),
                                        ALU.mult).then_inc(rope_k_parts, 1)
                for e in range(2):
                    nc.vector.tensor_tensor(ks[:, s, e, :], kk[:, :, 1 - e, :], sink[:, ts, e, :], ALU.mult
                                            ).then_inc(rope_k_parts, 1)
                nc.vector.tensor_tensor(kv[:, ts, ROT:], kv_in[:, ts, ROT:D], kv_in[:, ts, D + ROT:], ALU.mult
                                        ).then_inc(kv_pass_ready, 1)

            def norm_guard(i):
                dve.wait_ge(squares_done, 2 * i + 2)
                nc.vector.tensor_scalar(ssq_min[:, 2 * i:2 * i + 2], ssq[:, 2 * i:2 * i + 2], MIN_NORM * MIN_NORM,
                                        None, ALU.max).then_inc(ssq_min_ready, 1)

            def times_v(i):
                s = slice(2 * i % 4, 2 * i % 4 + 2)
                dve.wait_ge(rope_k_ready, i + 1)
                nc.vector.tensor_tensor(kv[:, 2 * i:2 * i + 2, 0:ROT],
                                        kr[:, s, :, :].rearrange("p t a d -> p t (a d)"),
                                        kv_in[:, 2 * i:2 * i + 2, D:D + ROT], ALU.mult).then_inc(kv_rot_ready, 1)

            def sum_kv(i):
                dve.wait_ge(kv_rot_ready, i + 1)
                dve.wait_ge(kv_pass_ready, i + 1)
                dve.wait_ge(rnorm_ready, i + 1)
                for e in range(2):
                    t = 2 * i + e
                    if i == 0:
                        nc.vector.tensor_scalar(kv_sum[:, e, :], kv[:, t, :], rnorm[:, t:t + 1], None, ALU.mult
                                                ).then_inc(kv_summed, 1)
                    else:
                        dve.wait_ge(kv_summed, t - 1)
                        nc.vector.scalar_tensor_tensor(kv_sum[:, e, :], kv[:, t, :], rnorm[:, t:t + 1],
                                                       kv_sum[:, e, :], ALU.mult, ALU.add).then_inc(kv_summed, 1)

            split_hm(0, 2)
            rope_k(0)
            norm_guard(0)
            dve.wait_ge(w_q_loaded, 16)
            nc.vector.tensor_copy(w_hi[:, :, 2 * D:], w_in[:, :, 2 * D:]).then_inc(w_hi_ready, 1)
            split_hm(0, 3)
            times_v(0)
            sum_kv(0)
            quantise(0, 0, 1)
            rope_k(1)
            norm_guard(1)
            times_v(1)
            sum_kv(1)
            rope_k(2)
            norm_guard(2)
            dve.wait_ge(g2_hi_ready, 1)
            dve.wait_ge(rows_ready, 2)
            nc.vector.tensor_tensor(g2_r[32:33, :], rows[32:33, 1, :], g2_r[32:33, :].bitcast(F32), ALU.subtract
                                    ).then_inc(g2_lo_ready, 1)
            dve.wait_ge(mod_summed, 5)
            nc.vector.tensor_copy(mod[:, SB, :], misc_cols(SB, CB)).then_inc(mod_b_ready, 1)
            nc.vector.tensor_scalar(scale2[:, :], misc_cols(CB, GB), 1.0, None, ALU.add).then_inc(mod_b_ready, 1)
            nc.vector.tensor_copy(mod[:, GB, :], misc_cols(GB, 6)).then_inc(mod_b_ready, 1)
            times_v(2)
            rope_k(3)
            norm_guard(3)
            threshold(1)

            def q_cos(h):
                dve.wait_ge(q_crossed, 2 * h + 2)
                nc.vector.scalar_tensor_tensor(qc[:, h, :], q_bank[h][0][:, :], bq[:, 0:1], cosq[:, cols(h)],
                                               ALU.add, ALU.mult).then_inc(qc_ready, 1)

            def q_sin(h):
                nc.vector.tensor_tensor(qx[:, h, :], qx[:, h, :], sinq[:, cols(h)], ALU.mult).then_inc(qs_ready, 1)

            for r in ropeq_loaded:
                dve.wait_ge(r, 16)
            sum_kv(2)
            times_v(3)
            q_cos(0)
            q_sin(0)
            dve.wait_ge(mod_b_ready, 3)
            gate(1, GB, 3)

            dve.wait_ge(a_summed, 1)
            nc.vector.tensor_copy(a[:, :], bank[6][:, 0:KC]).then_inc(a_ready, 1)
            dve.wait_ge(a_ready, 1)
            dve.wait_ge(w_out_loaded, 16)
            dve.wait_ge(rows_ready, 3)
            for k in range(KC):
                nc.vector.scalar_tensor_tensor(wa[:, k, :], w_out[:, k, :], a[:, k:k + 1], rows[:, 2, :],
                                               ALU.mult, ALU.mult).then_inc(wa_ready, 1)
            quantise(0, 1, 2)
            q_cos(1)
            q_sin(1)
            quantise(1, 0, 1)

            def add_y(i):
                dve.wait_ge(y_done, i + 1)
                dve.wait_ge(res_ready, i + 1)
                pair = x1[:, 2 * i:2 * i + 2, :].rearrange("p t d -> p (t d)")
                nc.vector.tensor_tensor(pair, y_bank[i][:, :], pair, ALU.add).then_inc(x1_ready, 1)
                dve.wait_ge(x1_ready, i + 1)

            add_y(0)
            norm_stats(1, 0)
            add_y(1)
            norm_stats(1, 1)
            threshold(2)
            quantise(1, 1, 2)
            norm_apply(1, 1)
            split_hm(1, 0)
            add_y(2)
            split_hm(1, 1)
            norm_stats(1, 2)
            add_y(3)
            norm_stats(1, 3)

            def product(n):
                h, j = ORDER[n]
                first, second = up_bank[n % 3]
                r = unit_rows(j)
                dve.wait_ge(sig_ready, n + 1)
                if n == 3:
                    dve.wait_ge(hid_lo0_ready, 1)
                if n > 3:
                    dve.wait_ge(hid_lo_ready, n - 3)
                src = second[:, :] if j < FULL else first[REST:P, :]
                nc.vector.tensor_tensor(hid[r, n % 3, :], src, sig[r, n % 3, :], ALU.mult).then_inc(hid_ready, 1)

            def hid_lo_part(n):
                h, j = ORDER[n]
                r = unit_rows(j)
                dve.wait_ge(hid_hi_ready, n + 1)
                lo = hid_lo[:, j, cols(h)] if j < FULL else hid_hi[REST:P, FULL, cols(h)]
                nc.vector.tensor_tensor(lo, hid[r, n % 3, :], hid_hi[r, j, cols(h)].bitcast(F32),
                                        ALU.subtract).then_inc(hid_lo_ready, 1)

            for n in range(len(ORDER)):
                product(n)
                if n == 0:
                    norm_apply(1, 3)
                if n == 3:
                    split_hm(1, 3)
                if n >= 2:
                    hid_lo_part(n - 1)
                if n == 1:
                    split_hm(1, 2)
                if n == 6:
                    quantise(2, 0, HC)
            hid_lo_part(len(ORDER) - 1)

            dve.wait_ge(rows_ready, 4)
            for t in range(TILES):
                dve.wait_ge(down_done, t + 1)
                nc.vector.tensor_tensor(x[:, t, :], down_bank[t][:, 0:D], rows[:, 3, :], ALU.mult
                                        ).then_inc(ffn_scaled, 1)
                dve.wait_ge(ffn_scaled, t + 1)
                nc.vector.tensor_tensor(x[:, t, :], x[:, t, :], x1[:, t, :], ALU.add).then_inc(out_ready, 1)

        @block.gpsimd
        def _(pool):
            nc.gpsimd.memset(minus_half[:, :], -0.5).then_inc(exponent_set, 1)
            nc.gpsimd.memset(ones[:, :], 1.0).then_inc(ones_set, 1)
            nc.gpsimd.memset(ones_r[:, :].bitcast(F32), 1.0).then_inc(ones_set, 1)

            def inv_std(layer, i):
                pool.wait_ge(var_ready, 2 * (layer * PAIRS + i + 1))
                pair = slice(2 * i, 2 * i + 2)
                nc.gpsimd.tensor_tensor(rstd[:, layer, pair], var_eps[:, layer, pair], minus_half[:, :], ALU.pow
                                        ).then_inc(rstd_ready, 1)
                pool.wait_ge(rstd_ready, layer * PAIRS + i + 1)
                nc.gpsimd.tensor_tensor(neg_mean_rstd[:, layer, pair], neg_mean[:, layer, pair], rstd[:, layer, pair],
                                        ALU.mult).then_inc(norm_ready, 1)

            pool.wait_ge(exponent_set, 1)
            inv_std(0, 0)
            inv_std(0, 1)

            def w_lo_part(n, cs):
                pool.wait_ge(w_hi_ready, n)
                nc.gpsimd.tensor_tensor(w_lo[:, :, cs], w_in[:, :, cs], w_hi[:, :, cs].bitcast(F32), ALU.subtract
                                        ).then_inc(w_lo_ready, 1)

            w_lo_part(1, slice(0, 2 * D))
            pool.wait_ge(brow_hi_ready, 1)
            pool.wait_ge(w_lo_ready, 1)
            nc.gpsimd.tensor_tensor(brow_r[32:33, :], brow[32:33, :], brow_r[32:33, :].bitcast(F32), ALU.subtract
                                    ).then_inc(brow_lo_ready, 1)
            pool.wait_ge(brow_lo_ready, 1)
            inv_std(0, 2)
            inv_std(0, 3)

            def residual(i, *steps):
                ts = slice(2 * i, 2 * i + 2)
                if 0 in steps:
                    if i == 0:
                        pool.wait_ge(rows_ready, 1)
                    pool.wait_ge(xn_ready, 2 * i + 2)
                    nc.gpsimd.tensor_tensor(x1[:, ts, :], xn[:, ts, :],
                                            rows[:, 0, :].unsqueeze(1).to_broadcast([P, 2, D]), ALU.mult
                                            ).then_inc(res_scaled, 1)
                if 1 in steps:
                    pool.wait_ge(res_scaled, i + 1)
                    nc.gpsimd.tensor_tensor(x1[:, ts, :], x1[:, ts, :], x[:, ts, :], ALU.add).then_inc(res_ready, 1)

            def rope_k_sum(i):
                s = slice(2 * i % 4, 2 * i % 4 + 2)
                pool.wait_ge(rope_k_parts, 3 * (i + 1))
                if i >= 2:
                    pool.wait_ge(kv_rot_ready, i - 1)
                nc.gpsimd.tensor_tensor(kr[:, s, :, :], kc[:, s, :, :], ks[:, s, :, :], ALU.add
                                        ).then_inc(rope_k_ready, 1)

            def inv_norm(i):
                pool.wait_ge(ssq_min_ready, i + 1)
                nc.gpsimd.tensor_tensor(rnorm[:, 2 * i:2 * i + 2], ssq_min[:, 2 * i:2 * i + 2],
                                        minus_half[:, :], ALU.pow).then_inc(rnorm_ready, 1)

            def q_sum(h):
                pool.wait_ge(qc_ready, h + 1)
                pool.wait_ge(qs_ready, h + 1)
                nc.gpsimd.tensor_tensor(q[:, 0, cols(h)], qc[:, h, :], qx[:, h, :], ALU.add).then_inc(q_rot_ready, 1)

            def flags_below(i):
                pool.wait_ge(thr_ready, 2 * i + 2)
                nc.gpsimd.tensor_scalar(below(i), (w1, w2, w3)[i][:, :, :], nthr[:, i:i + 1], None, ALU.is_lt
                                        ).then_inc((w1_below_ready, w2_below_ready, w3_below_ready)[i], 1)

            pool.wait_ge(abs_done, 1)
            flags_below(0)
            rope_k_sum(0)
            inv_norm(0)
            w_lo_part(2, slice(2 * D, 3 * D))
            residual(0, 0)
            rope_k_sum(1)
            inv_norm(1)
            residual(0, 1)
            rope_k_sum(2)
            inv_norm(2)
            residual(1, 0)
            rope_k_sum(3)
            inv_norm(3)
            pool.wait_ge(kv_summed, TILES - 2)
            nc.gpsimd.tensor_tensor(kv_sum[:, 0, :], kv_sum[:, 0, :], kv_sum[:, 1, :], ALU.add
                                    ).then_inc(kv_total_ready, 1)
            residual(1, 1)
            q_sum(0)
            residual(2, 0)
            q_sum(1)
            residual(2, 1)
            inv_std(1, 0)
            residual(3, 0)
            inv_std(1, 1)
            residual(3, 1)
            pool.wait_ge(quant_ready, KC)
            flags_below(2)
            inv_std(1, 2)
            inv_std(1, 3)
            pool.wait_ge(hid_hi_ready, 1)
            nc.gpsimd.tensor_tensor(hid_lo[:, 0, cols(0)], hid[:, 0, :], hid_hi[:, 0, cols(0)].bitcast(F32),
                                    ALU.subtract).then_inc(hid_lo0_ready, 1)
            pool.wait_ge(hm_hi_ready, PAIRS + 3)
            nc.gpsimd.tensor_tensor(hm_lo[:, :, pair_cols(2)], hm[:, :, pair_cols(2)],
                                    hm_hi[:, :, pair_cols(2)].bitcast(F32), ALU.subtract).then_inc(hm_lo_pool_ready, 1)

        @block.tensor
        def _(pe):
            def mod_columns(v0, v1):
                for m in range(v0 * KC, v1 * KC):
                    for k in range(KC):
                        last = nc.tensor.matmul(misc[:, MOD0 + m:MOD0 + m + 1], wm[:, k, m * P:(m + 1) * P],
                                                silu_c[:, k:k + 1], start=(k == 0), stop=(k == KC - 1))
                last.then_inc(mod_summed, 1)

            def turn(layer, i, first=False):
                if first:
                    pe.wait_ge(ident_loaded, 16)
                pe.wait_ge(xn_ready, layer * TILES + 2 * i + 2)
                for k in range(KC):
                    for e in range(2):
                        at = (k * 2 + e) * P
                        last = nc.tensor.transpose(turn_bank[layer][i][:, at:at + P],
                                                   xn[:, 2 * i + e, k * P:(k + 1) * P], ident[:, :])
                last.then_inc(turned, 1)

            def kv_tiles(*tiles):
                def term(t, x_part, w_part, first=False):
                    for k in range(KC):
                        nc.tensor.matmul(kv_bank[t][:, :], x_part[:, k, t * P:(t + 1) * P], w_part[:, k, 0:2 * D],
                                         start=(first and k == 0), stop=False)

                for t in tiles:
                    if t in (2, 3):
                        pe.wait_ge(hm_ready, KC * (t - 1))
                    if t >= 4:
                        pe.wait_ge(kv_in_ready, t - 3)
                    pe.wait_ge(hm_hi_ready, t // 2 + 1)
                    pe.wait_ge(w_hi_ready, 1)
                    term(t, hm_hi, w_hi, first=True)
                for t in tiles:
                    pe.wait_ge(hm_lo_ready, t // 2 + 1)
                    term(t, hm_lo, w_hi)
                for t in tiles:
                    pe.wait_ge(w_lo_ready, 1)
                    term(t, hm_hi, w_lo)
                    pe.wait_ge(brow_lo_ready, 1)
                    nc.tensor.matmul(kv_bank[t][:, :], ones_r[:, 0:P], brow_r[:, :], start=False, stop=True
                                     ).then_inc(kv_done, 1)

            def spread(dst, r):
                for k in range(KC):
                    last = nc.tensor.transpose(dst[:, k * P:(k + 1) * P],
                                               rows_src[:, r, k:k + 1].to_broadcast([P, P]), ident[:, :])
                return last

            def gamma(i):
                pe.wait_ge(abs_done, i + 1)
                if i > 0:
                    pe.wait_ge(thr_ready, 2 * i)
                g = misc[:, G0 + i:G0 + i + 1]
                if i < 2:
                    nc.tensor.matmul(g, ones[:, :], abs_sum[:, i:i + 1], start=True, stop=True
                                     ).then_inc(gamma_summed, 1)
                else:
                    pe.wait_ge(abs_done, 4)
                    nc.tensor.matmul(g, ones[:, :], abs_sum[:, 2:3], start=True, stop=False)
                    nc.tensor.matmul(g, ones[0:REST, :], abs_sum[0:REST, 3:4], start=False, stop=True
                                     ).then_inc(gamma_summed, 1)

            def a_columns():
                pe.wait_ge(g2_hi_ready, 1)
                pe.wait_ge(kv_rot_ready, PAIRS)
                pe.wait_ge(kv_pass_ready, PAIRS)
                pe.wait_ge(rnorm_ready, PAIRS)
                terms = [(kv[:, t, :], rnorm[:, t:t + 1]) for t in (TILES - 2, TILES - 1)]
                terms += [(kv_sum[:, 0, :], ones[:, 0:1])]
                for i, (products, weights) in enumerate(terms):
                    if i == 2:
                        pe.wait_ge(kv_total_ready, 1)
                    for m in range(KC):
                        last = nc.tensor.matmul(bank[6][:, m:m + 1], products[:, m * P:(m + 1) * P], weights,
                                                start=(i == 0 and m == 0), stop=(i == 2 and m == KC - 1))
                last.then_inc(a_summed, 1)

            def keep_warm(dst, n):
                for _ in range(n):
                    nc.tensor.matmul(dst[:, :], ones_r[:, 0:P], ones_r[:, :], start=True, stop=True)

            pe.wait_ge(ones_set, 2)
            keep_warm(bank[6], WARM_UP)
            pe.wait_ge(silu_ready, 1)
            pe.wait_ge(wm_a_loaded, 16)
            mod_columns(SA, GA)
            turn(0, 0, first=True)
            keep_warm(bank[6], KEEP_WARM)
            turn(0, 1)
            kv_tiles(0, 1)
            pe.wait_ge(wm_ga_loaded, 16)
            pe.wait_ge(mod_a_ready, 2)
            mod_columns(GA, SB)
            gamma(0)
            turn(0, 2)
            kv_tiles(2)
            turn(0, 3)
            pe.wait_ge(rows_src_ready, 2)
            spread(bank[6][:, 0:D], 0)
            spread(bank[6][:, D:2 * D], 1).then_inc(rows_spread, 1)
            kv_tiles(3)
            kv_tiles(4)
            pe.wait_ge(hm_ready, KC * PAIRS)
            spread(bank[3][:, 0:D], 2).then_inc(rows_spread, 1)
            kv_tiles(5)
            pe.wait_ge(wm_b_loaded, 16)
            pe.wait_ge(mod_ga_ready, 1)
            pe.wait_ge(thr_ready, 2)
            mod_columns(SB, CB)
            kv_tiles(6)
            mod_columns(CB, GB)
            kv_tiles(7)
            mod_columns(GB, 6)

            def q_part(h, m, done):
                cs = slice(2 * D + m * P, 2 * D + (m + 1) * P)
                terms = [(w_hi, hm_hi), (w_hi, hm_lo), (w_lo, hm_hi)]
                for i, (w, t) in enumerate(terms):
                    if i == 2:
                        pe.wait_ge(w_lo_ready, 2)
                    for k in range(KC):
                        last = nc.tensor.matmul(q_bank[h][m][:, :], w[:, k, cs], t[:, k, cols(h)],
                                                start=(i == 0 and k == 0), stop=(i == 2 and k == KC - 1))
                last.then_inc(done, 1)

            pe.wait_ge(w_hi_ready, 2)
            q_part(0, 0, q_rot_done)
            pe.wait_ge(mod_b_ready, 3)
            gamma(1)
            pe.wait_ge(rows_ready, 3)
            q_part(0, 1, q_pass_done)
            pe.wait_ge(kv_in_ready, 6)
            q_part(1, 0, q_rot_done)
            a_columns()
            q_part(1, 1, q_pass_done)
            pe.wait_ge(gate_ready, 2)
            pe.wait_ge(thr_ready, 4)
            spread(misc[:, GB_ROW:GB_ROW + D], 3).then_inc(rows_spread, 1)

            def y_pair(i, *tiles):
                if i < 2:
                    pe.wait_ge(kv_in_ready, TILES)
                if i == 3:
                    pe.wait_ge(qc_ready, 1)
                pe.wait_ge(q_rot_ready, i // 2 + 1)
                pe.wait_ge(q_pass_ready, i // 2 + 1)
                if 0 in tiles:
                    nc.tensor.matmul(y_bank[i][:, :], two_rows[:, :], g2_r[:, :].unsqueeze(1).to_broadcast([33, 2, D]),
                                     start=True, stop=False)
                for e in tiles:
                    for k in range(KC):
                        t = 2 * i + e
                        last = nc.tensor.matmul(y_bank[i][:, e * D:(e + 1) * D], q[:, k, t * P:(t + 1) * P],
                                                wa[:, k, :], start=False, stop=(e == 1 and k == KC - 1))
                if 1 in tiles:
                    last.then_inc(y_done, 1)

            pe.wait_ge(wa_ready, KC)
            pe.wait_ge(selector_set, 2)
            pe.wait_ge(g2_lo_ready, 1)
            for i in range(3):
                y_pair(i, 0, 1)
            pe.wait_ge(rows_ready, 4)
            gamma(2)
            turn(1, 0)
            y_pair(3, 0)
            pe.wait_ge(x1_ready, 1)
            turn(1, 1)
            y_pair(3, 1)

            def up(n, cs):
                h, j = ORDER[n]
                if n >= 3:
                    pe.wait_ge(hid_ready, n - 2)
                if n == 2:
                    pe.wait_ge(x1_ready, 4)
                    pe.wait_ge(hm_ready, KC * (PAIRS + 1))
                c0 = (j * P, (FULL + 1 + j) * P)
                for m in range(2 if j < FULL else 1):
                    for i, t in enumerate((hm_hi, hm_lo)):
                        if n == HC and i == 1:
                            pe.wait_ge(hm_lo_pool_ready, 1)
                            pe.wait_ge(hm_lo_ready, 2 * PAIRS - 1)
                        for k in range(KC):
                            last = nc.tensor.matmul(up_bank[n % 3][m][:, cs], w12q[:, k, c0[m]:c0[m] + P],
                                                    t[:, k, h * N + cs.start:h * N + cs.stop],
                                                    start=(i == 0 and k == 0), stop=(i == 1 and k == KC - 1))
                return last

            pe.wait_ge(quant_ready, 2 * KC)
            pe.wait_ge(hm_lo_ready, PAIRS + 1)
            pe.wait_ge(qc_ready, 2)
            up(0, slice(0, 2 * P))
            pe.wait_ge(thr_ready, 6)
            pe.wait_ge(x1_ready, 3)
            up(1, slice(0, 2 * P))
            pe.wait_ge(hm_lo_ready, PAIRS + 2)
            for n in range(2):
                up(n, slice(2 * P, 4 * P)).then_inc(up_done, 1)
            for n in range(2, len(ORDER)):
                if n == 3:
                    pe.wait_ge(x1_ready, 2)
                    turn(1, 2)
                if n == 4:
                    pe.wait_ge(hm_ready, KC * (PAIRS + 2))
                    turn(1, 3)
                if n == HC:
                    pe.wait_ge(hm_hi_ready, 2 * PAIRS)
                up(n, slice(0, N)).then_inc(up_done, 1)

            pe.wait_ge(quant_ready, 2 * KC + 1)
            pe.wait_ge(hm_ready, KC * 2 * PAIRS)
            for t in range(TILES):
                if t == 2:
                    pe.wait_ge(hid_ready, len(ORDER) - 2)
                if t == 4:
                    pe.wait_ge(hid_ready, len(ORDER) - 1)
                if t == 6:
                    pe.wait_ge(hid_ready, len(ORDER))
                for j in range(HC):
                    n = HC * (t // (TILES // NH)) + j
                    pe.wait_ge(hid_hi_ready, n + 1)
                    if j == FULL:
                        pe.wait_ge(hid_lo_ready, n)
                    last = nc.tensor.matmul(down_bank[t][:, 0:D], hid_hi[:, j, t * P:(t + 1) * P], w3q[:, j, :],
                                            start=(j == 0), stop=(j == FULL))
                    if j < FULL:
                        if n == 0:
                            pe.wait_ge(hid_lo0_ready, 1)
                        else:
                            pe.wait_ge(hid_lo_ready, n)
                        nc.tensor.matmul(down_bank[t][:, 0:D], hid_lo[:, j, t * P:(t + 1) * P], w3q[:, j, :],
                                         start=False, stop=False)
                last.then_inc(down_done, 1)


def rope_tables():
    inv_freq = (np.float32(1.0) / np.float32(10000.0) ** (np.arange(0, ROT, 2, dtype=np.float32) / np.float32(ROT)))
    freqs = np.arange(S, dtype=np.float32)[:, None] * inv_freq.astype(np.float32)[None, :]
    return np.cos(freqs).astype(np.float32), np.sin(freqs).astype(np.float32)


def kernel(**inputs):
    import concourse.bacc as bacc
    from concourse.bass_utils import run_bass_kernel_spmd

    g = {n: np.asarray(v) for n, v in inputs.items()}
    order = np.concatenate([np.arange(0, ROT, 2), np.arange(1, ROT, 2), np.arange(ROT, D)])
    rows_q, rows_k, rows_v = order, D + order, 2 * D + order
    kvq = np.concatenate([rows_k, rows_v, rows_q])
    cos, sin = rope_tables()
    token = np.arange(S).reshape(P, TILES).T.reshape(-1)
    hid2 = np.concatenate([np.arange(FULL * P, HID), np.arange(FULL * P)])
    arrays = {
        "x_in": g["L0_attn_X"][0],
        "w_in_t": g["L0_attn_W_in"][kvq].T,
        "b_in": g["L0_attn_b_in"][kvq][None, :],
        "b_q_cols": g["L0_attn_b_in"][rows_q].reshape(KC, P).T,
        "w_out_t": g["L0_attn_W_out"].T[order],
        "b_out_cols": g["L0_attn_b_out"].reshape(KC, P).T,
        "w1_t": g["L0_ffn_w1"].T,
        "w2_t": g["L0_ffn_w2"][hid2].T,
        "w3_t": g["L0_ffn_w3"].T,
        "c_cols": g["L0_c"].reshape(KC, P).T,
        "wmod": g["L0_wmod"],
        "cos_tok": cos,
        "sin_tok": np.concatenate([-sin, sin], axis=1),
        "cos_feat": np.concatenate([cos[token].T, cos[token].T], axis=0),
        "sin_feat": np.concatenate([-sin[token].T, sin[token].T], axis=0),
        "ident_in": np.eye(P, dtype=np.float32),
    }
    arrays = {n: np.ascontiguousarray(v) for n, v in arrays.items()}
    nc = bacc.Bacc("TRN2", target_bir_lowering=False, num_devices=1)
    args = [nc.dram_tensor(n, v.shape, mybir.dt.from_np(v.dtype), kind="ExternalInput").ap()
            for n, v in arrays.items()]
    out = nc.dram_tensor("out", (S, D), F32, kind="ExternalOutput").ap()
    adaln_block(nc, *args, out)
    r = run_bass_kernel_spmd(nc, [arrays], core_ids=[0])
    return np.asarray(r.results[0]["out"]).reshape(1, S, D)
```
